# Optimizing a Trainium2 kernel written in Bass

```python
import numpy as np
import jax
import jax.numpy as jnp

def _softmax(x, axis=-1):
    return jax.nn.softmax(x, axis=axis)
def _gelu(x):
    return jax.nn.gelu(x, approximate=True)
def _silu(x):
    return jax.nn.silu(x)
def _sigmoid(x):
    return jax.nn.sigmoid(x)
def _layernorm(x, axis=-1, eps=1e-5):
    m = jnp.mean(x, axis=axis, keepdims=True)
    v = jnp.var(x, axis=axis, keepdims=True)
    return (x - m) / jnp.sqrt(v + eps)
def _scatter_add(tgt, idx, src, axis=0):
    return tgt.at[idx].add(src)
def _segment_sum(src, seg, n):
    return jax.ops.segment_sum(src, seg, n)

kernel_name = 'mk_adj_resnorm_d2_adj_128_96ebb4'

def setup_inputs(seed: int = 0):
    np.random.seed(seed)
    _w = jnp.asarray
    def _rec_inputs():
        import jax
        import jax.numpy as jnp
        _gk = jax.random.key(seed)
        x = -0.000929 + 1 * jax.random.normal(jax.random.fold_in(_gk, 1), (8192, 128), jnp.float32)
        _a = jax.random.bernoulli(jax.random.fold_in(_gk, 2), 0.000976562, (8192, 8192))
        _a = jnp.logical_or(_a, jnp.swapaxes(_a, -1, -2))
        _a = jnp.logical_or(_a, jnp.eye(8192, dtype=bool))
        _af = _a.astype(jnp.float32)
        adj = _af
        return x, adj
    x, adj = _rec_inputs()
    def _L0_gnn_setup():
        import jax, jax.numpy as jnp
        import numpy as np
        N, EMB, HID = (8192, 128, 128)
        key = jax.random.key(seed)
        k1, k2, k3, k4, k5, k6, k7, k8 = jax.random.split(key, 8)
        inlayer = jax.random.normal(k1, (N, EMB), dtype=jnp.float32)
        inlayer2 = jax.random.normal(k2, (N, 2 * EMB), dtype=jnp.float32)
        adj_mat = jax.random.randint(k3, (N, N), 0, 2).astype(jnp.float32)
        W1 = jax.random.normal(k4, (HID, 2 * EMB), dtype=jnp.float32) / np.sqrt(2 * EMB)
        w2 = jax.random.normal(k5, (HID,), dtype=jnp.float32) / np.sqrt(HID)
        b2 = jax.random.normal(k6, (), dtype=jnp.float32) * 0.01
        w3 = jax.random.normal(k7, (HID,), dtype=jnp.float32) / np.sqrt(HID)
        b3 = jax.random.normal(k8, (), dtype=jnp.float32) * 0.01
        return {'inlayer': inlayer, 'inlayer2': inlayer2, 'adj_mat': adj_mat, 'W1': W1, 'w2': w2, 'b2': b2, 'w3': w3, 'b3': b3}
    _L0_gnn_all = _L0_gnn_setup()
    _L0_gnn_in = {k: v for k, v in _L0_gnn_all.items() if k in ('inlayer2', 'W1', 'w2', 'b2', 'w3', 'b3', )}
    del _L0_gnn_all

    def _L1_gnn_setup():
        import jax, jax.numpy as jnp
        import numpy as np
        N, IN, H, C = (4096, 128, 4, 32)
        HC = H * C
        EDGE_P = 0.008

        def _linear_params(key, fan_in, fan_out, bias=True):
            k1, k2 = jax.random.split(key)
            lim = 1.0 / np.sqrt(fan_in)
            W = jax.random.uniform(k1, (fan_in, fan_out), jnp.float32, -lim, lim)
            if not bias:
                return W
            b = jax.random.uniform(k2, (fan_out,), jnp.float32, -lim, lim)
            return (W, b)

        def _transformer_conv(x, adj, Wq, bq, Wk, bk, Wv, bv, Ws, bs, Wb):
            n = x.shape[0]
            q = (x @ Wq + bq).reshape(n, H, C)
            k = (x @ Wk + bk).reshape(n, H, C)
            v = (x @ Wv + bv).reshape(n, H, C)
            attn = jnp.einsum('nhc,mhc->hnm', q, k) / np.float32(np.sqrt(C))
            mask = adj == 0.0
            neg = jnp.where(mask[None], -jnp.inf, attn)
            m = jnp.max(neg, axis=-1, keepdims=True)
            all_inf = jnp.isneginf(m)
            e = jnp.where(mask[None], 0.0, jnp.exp(neg - jnp.where(all_inf, 0.0, m)))
            denom = jnp.sum(e, axis=-1, keepdims=True)
            alpha = e / jnp.where(denom == 0.0, 1.0, denom)
            out = jnp.einsum('hnm,mhc->hnc', alpha, v)
            out = jnp.transpose(out, (1, 2, 0)).reshape(n, C * H)
            x_r = x @ Ws + bs
            beta = jax.nn.sigmoid(jnp.concatenate([out, x_r, out - x_r], axis=-1) @ Wb)
            return beta * x_r + (1.0 - beta) * out
        key = jax.random.key(seed)
        ks = jax.random.split(key, 7)
        x = jax.random.normal(ks[0], (N, IN), jnp.float32)
        adj = (jax.random.uniform(ks[1], (N, N)) < EDGE_P).astype(jnp.float32)
        Wq, bq = _linear_params(ks[2], IN, HC)
        Wk, bk = _linear_params(ks[3], IN, HC)
        Wv, bv = _linear_params(ks[4], IN, HC)
        Ws, bs = _linear_params(ks[5], IN, HC)
        Wb = _linear_params(ks[6], 3 * HC, 1, bias=False)
        return dict(x=x, adj=adj, Wq=Wq, bq=bq, Wk=Wk, bk=bk, Wv=Wv, bv=bv, Ws=Ws, bs=bs, Wb=Wb)
    _L1_gnn_all = _L1_gnn_setup()
    _L1_gnn_in = {k: v for k, v in _L1_gnn_all.items() if k in ('Wq', 'bq', 'Wk', 'bk', 'Wv', 'bv', 'Ws', 'bs', 'Wb', )}
    del _L1_gnn_all

    return {
        "x": x,
        "adj": adj,
        "L0_gnn_inlayer2": _L0_gnn_in["inlayer2"],
        "L0_gnn_W1": _L0_gnn_in["W1"],
        "L0_gnn_w2": _L0_gnn_in["w2"],
        "L0_gnn_b2": _L0_gnn_in["b2"],
        "L0_gnn_w3": _L0_gnn_in["w3"],
        "L0_gnn_b3": _L0_gnn_in["b3"],
        "L1_gnn_Wq": _L1_gnn_in["Wq"],
        "L1_gnn_bq": _L1_gnn_in["bq"],
        "L1_gnn_Wk": _L1_gnn_in["Wk"],
        "L1_gnn_bk": _L1_gnn_in["bk"],
        "L1_gnn_Wv": _L1_gnn_in["Wv"],
        "L1_gnn_bv": _L1_gnn_in["bv"],
        "L1_gnn_Ws": _L1_gnn_in["Ws"],
        "L1_gnn_bs": _L1_gnn_in["bs"],
        "L1_gnn_Wb": _L1_gnn_in["Wb"],
    }

def reference(x, adj, L0_gnn_inlayer2, L0_gnn_W1, L0_gnn_w2, L0_gnn_b2, L0_gnn_w3, L0_gnn_b3, L1_gnn_Wq, L1_gnn_bq, L1_gnn_Wk, L1_gnn_bk, L1_gnn_Wv, L1_gnn_bv, L1_gnn_Ws, L1_gnn_bs, L1_gnn_Wb):
    import jax
    import jax.numpy as jnp
    def _L0_gnn_ref(inlayer, inlayer2, adj_mat, W1, w2, b2, w3, b3):
        import jax, jax.numpy as jnp
        import numpy as np
        N, EMB, HID = (8192, 128, 128)
        in_fts = jnp.einsum('ne,he->nh', inlayer2, W1)
        f1 = in_fts @ w2 + b2
        f2 = in_fts @ w3 + b3
        logits = f1[:, None] + f2[None, :]
        logits = adj_mat * logits
        bias_mat = -1000000000.0 * (1.0 - (adj_mat > 0).astype(jnp.float32))
        coefs = jax.nn.softmax(jax.nn.leaky_relu(logits, 0.01) + bias_mat, axis=1)
        vals = coefs @ inlayer
        return vals

    def _L1_gnn_ref(x, adj, Wq, bq, Wk, bk, Wv, bv, Ws, bs, Wb):
        import jax, jax.numpy as jnp
        import numpy as np
        N, IN, H, C = (4096, 128, 4, 32)
        HC = H * C
        EDGE_P = 0.008

        def _linear_params(key, fan_in, fan_out, bias=True):
            k1, k2 = jax.random.split(key)
            lim = 1.0 / np.sqrt(fan_in)
            W = jax.random.uniform(k1, (fan_in, fan_out), jnp.float32, -lim, lim)
            if not bias:
                return W
            b = jax.random.uniform(k2, (fan_out,), jnp.float32, -lim, lim)
            return (W, b)

        def _transformer_conv(x, adj, Wq, bq, Wk, bk, Wv, bv, Ws, bs, Wb):
            n = x.shape[0]
            q = (x @ Wq + bq).reshape(n, H, C)
            k = (x @ Wk + bk).reshape(n, H, C)
            v = (x @ Wv + bv).reshape(n, H, C)
            attn = jnp.einsum('nhc,mhc->hnm', q, k) / np.float32(np.sqrt(C))
            mask = adj == 0.0
            neg = jnp.where(mask[None], -jnp.inf, attn)
            m = jnp.max(neg, axis=-1, keepdims=True)
            all_inf = jnp.isneginf(m)
            e = jnp.where(mask[None], 0.0, jnp.exp(neg - jnp.where(all_inf, 0.0, m)))
            denom = jnp.sum(e, axis=-1, keepdims=True)
            alpha = e / jnp.where(denom == 0.0, 1.0, denom)
            out = jnp.einsum('hnm,mhc->hnc', alpha, v)
            out = jnp.transpose(out, (1, 2, 0)).reshape(n, C * H)
            x_r = x @ Ws + bs
            beta = jax.nn.sigmoid(jnp.concatenate([out, x_r, out - x_r], axis=-1) @ Wb)
            return beta * x_r + (1.0 - beta) * out
        return _transformer_conv(x, adj, Wq, bq, Wk, bk, Wv, bv, Ws, bs, Wb)

    x = _layernorm(x + _L0_gnn_ref(x, L0_gnn_inlayer2, adj, L0_gnn_W1, L0_gnn_w2, L0_gnn_b2, L0_gnn_w3, L0_gnn_b3), axis=-1)
    x = _layernorm(x + _L1_gnn_ref(x, adj, L1_gnn_Wq, L1_gnn_bq, L1_gnn_Wk, L1_gnn_bk, L1_gnn_Wv, L1_gnn_bv, L1_gnn_Ws, L1_gnn_bs, L1_gnn_Wb), axis=-1)
    return x


_drawn_inputs = setup_inputs


def setup_inputs(seed=0):
    import zlib

    import numpy as np

    out = dict(_drawn_inputs(seed))
    spreads = {}
    factors = {'L1_gnn_bq': 25.753, 'L1_gnn_bk': 64.0}
    for name, (base, spread) in spreads.items():
        noise = np.random.default_rng([zlib.crc32(name.encode()), seed]).standard_normal(out[name].shape)
        drawn = base * np.exp(spread * noise) if base else spread * noise
        out[name] = jnp.asarray(drawn.astype(out[name].dtype))
    for name, factor in factors.items():
        out[name] = (out[name] * factor).astype(out[name].dtype)
    return out
```

```python
from contextlib import ExitStack

import concourse.bass as bass
import concourse.mybir as mybir
from concourse.alu_op_type import AluOpType as ALU

F32 = mybir.dt.float32
BF16 = mybir.dt.bfloat16
FP16 = mybir.dt.float16
I32 = mybir.dt.int32
ACT = mybir.ActivationFunctionType
AX = mybir.AxisListType

P = 128
N = 8192
D = 128
HEADS = 4
C = D // HEADS
TILES = N // P
TPC = 4
CHUNK = TPC * P
CHUNKS = N // CHUNK
PAIRS = TILES // 2
PAIR_W = 2 * CHUNK
ONE = D + 1
SLOPE = 0.01
EPS = 1e-5
SCALE = float(C) ** -0.5
RSQRT_MAGIC = 1597463007.0
VW = 64
KROWS = 3 * C + 1


class Chain:

    def __init__(self, eng, sem, start=0):
        self.eng, self.sem, self.n = eng, sem, start
        self.steps = 0

    def __call__(self, ins):
        ins.then_inc(self.sem, 1)
        self.n = self.n + 1
        self.steps += 1
        self.eng.wait_ge(self.sem, self.n)


def wait_apart(eng, sem, value, mark):
    eng.wait_ge(sem, value)
    eng.sem_inc(mark, 1)


def bcast(ap, shape):
    return ap.to_broadcast(shape)


def rsqrt_newton(chain, dve, out, v, tmp):
    chain(dve.tensor_scalar(out.bitcast(I32), v.bitcast(I32), -0.5, RSQRT_MAGIC, ALU.mult, ALU.add))
    for _ in range(4):
        chain(dve.tensor_tensor(tmp, out, out, ALU.mult))
        chain(dve.tensor_tensor(tmp, tmp, v, ALU.mult))
        chain(dve.tensor_scalar(tmp, tmp, -0.5, 1.5, ALU.mult, ALU.add))
        chain(dve.tensor_tensor(out, out, tmp, ALU.mult))


RSQRT_STEPS = 17


def node_logits(nc, io, G):
    GT = 8
    NG = TILES // GT
    with ExitStack() as ctx:
        sb = lambda n, s, d=F32: ctx.enter_context(nc.sbuf_tensor(n, s, d))
        ps = lambda n, s, d=F32: ctx.enter_context(nc.psum_tensor(n, s, d))
        sem = lambda n: ctx.enter_context(nc.semaphore(n))
        inl = sb("inl", [P, 2, GT, 2 * D])
        junk = sb("junk", [P, 4, 2 * D])
        W1 = sb("W1", [P, 2 * D])
        wcol = sb("wcol", [P, 2])
        bcol = sb("bcol", [P, 2])
        wrow = sb("wrow", [P, 2, P])
        ub = sb("ub", [P, 2, 2 * D])
        f = sb("f", [P, 2, TILES])
        s = sb("s", [P, TILES])
        s_small = sb("s_small", [P, TILES])
        s_max = sb("s_max", [P, TILES])
        gmax = sb("gmax", [P, 4])
        diag = sb("diag", [P, 2, CHUNK])
        u_ps = ps("u_ps", [P, 2, 2 * D])
        f_ps = ps("f_ps", [P, 2, CHUNK])
        weights_in, inl_in0, inl_in1 = sem("weights_in"), sem("inl_in0"), sem("inl_in1")
        inl_in = [inl_in0, inl_in1]
        dots_done, consts_ready, wrow_ready, u_done, ub_ready = (
            sem("dots_done"), sem("consts_ready"), sem("wrow_ready"), sem("u_done"), sem("ub_ready"))
        dve_step, act_step, pool_step = sem("dve_step"), sem("act_step"), sem("pool_step")
        f_ready, gpart_ready, gmax_ready, args_ready = (
            sem("f_ready"), sem("gpart_ready"), sem("gmax_ready"), sem("args_ready"))
        diag_ready, f_bcast, f_copied = sem("diag_ready"), sem("f_bcast"), sem("f_copied")
        block = ctx.enter_context(nc.Block())

        @block.sync
        def _(sp):
            sp.dma_start(W1[:], io["W1"]).then_inc(weights_in, 16)
            for i, k in enumerate(("w2", "w3")):
                sp.dma_start(wcol[:, i:i + 1], io[k].rearrange("(p a) -> p a", a=1)).then_inc(weights_in, 16)
            for i, k in enumerate(("b2", "b3")):
                sp.dma_start(bcol[:, i:i + 1], io[k].partition_broadcast(P).rearrange("p a b -> p (a b)")
                             ).then_inc(weights_in, 16)
            src = io["inl"].rearrange("(p g t) f -> g p (t f)", p=P, g=NG)
            with sp.Fori(0, NG // 2) as gg:
                for b in range(2):
                    sp.wait_ge(dots_done, (2 * gg + b) * (2 * GT) + 2 * GT)
                    sp.dma_start(inl[:, b].rearrange("p t f -> p (t f)"),
                                 src[bass.ds(2 * gg + b, 1)].rearrange("a p w -> (a p) w")).then_inc(inl_in[b], 16)

        @block.gpsimd
        def _(pool):
            chain = Chain(pool, pool_step)
            chain(pool.memset(G["ident"][:], 0.0))
            pool.affine_select(out=G["ident"][:], in_=G["ident"][:], compare_op=ALU.not_equal, fill=1.0,
                               base=0, pattern=[[-1, P]], channel_multiplier=1).then_inc(consts_ready, 1)
            pool.memset(G["ones"][:], 1.0).then_inc(consts_ready, 1)
            pool.memset(G["zeros"][:], 0.0).then_inc(consts_ready, 1)
            pool.wait_ge(gpart_ready, 1)
            pool.partition_all_reduce(gmax[:, 1:2], gmax[:, 0:1], P, bass.bass_isa.ReduceOp.max
                                      ).then_inc(gmax_ready, 1)

        @block.vector
        def _(dve):
            chain = Chain(dve, dve_step)
            dve.wait_ge(weights_in, 5 * 16)
            dve.wait_ge(consts_ready, 3)
            for i in range(2):
                dve.tensor_scalar(wrow[:, i], G["ones"][:], wcol[:, i:i + 1], None, ALU.mult
                                  ).then_inc(wrow_ready, 1)
            dve.sem_inc(dots_done, 4 * GT)
            dve.wait_ge(ub_ready, 1)
            with dve.Fori(0, NG // 2) as gg:
                for b in range(2):
                    dve.wait_ge(inl_in[b], gg * 16 + 16)
                    for k in range(2 * GT):
                        t, i = k // 2, k % 2
                        dve.wait_ge(dots_done, (2 * gg + b) * (2 * GT) + k + 4 * GT - 3)
                        dve.scalar_tensor_tensor(
                            out=junk[:, k % 4], in0=inl[:, b, t], scalar=1.0, in1=ub[:, i], op0=ALU.mult,
                            op1=ALU.mult, accum_out=f[:, i, bass.ds((2 * gg + b) * GT + t, 1)]
                        ).then_inc(dots_done, 1)
            dve.wait_ge(dots_done, 2 * TILES + 4 * GT)
            dve.tensor_scalar(G["f1"][:], f[:, 0], bcol[:, 0:1], None, ALU.add).then_inc(f_ready, 1)
            chain(dve.tensor_scalar(f[:, 1], f[:, 1], bcol[:, 1:2], None, ALU.add))
            dve.reduce_max(gmax[:, 0:1], f[:, 1], AX.X).then_inc(gpart_ready, 1)
            dve.tensor_scalar(G["neg_f2"][:], f[:, 1], -1.0, None, ALU.mult)
            dve.wait_ge(gmax_ready, 1)
            dve.wait_ge(f_ready, 1)
            chain(dve.tensor_scalar(s[:], G["f1"][:], gmax[:, 1:2], None, ALU.add))
            chain(dve.tensor_scalar(s_small[:], s[:], SLOPE, None, ALU.mult))
            chain(dve.tensor_tensor(s_max[:], s[:], s_small[:], ALU.max))
            chain(dve.tensor_tensor(s[:], s[:], s_max[:], ALU.subtract))
            chain(dve.tensor_tensor(s_small[:], s_small[:], s_max[:], ALU.subtract))
            chain(dve.tensor_scalar(gmax[:, 2:3], gmax[:, 1:2], -1.0, None, ALU.mult))
            dve.tensor_scalar(gmax[:, 3:4], gmax[:, 1:2], -SLOPE, None, ALU.mult).then_inc(args_ready, 1)
            dve.sem_inc(f_copied, 2)
            with dve.Fori(0, CHUNKS // 2) as cc:
                for b in range(2):
                    c = 2 * cc + b
                    dve.wait_ge(f_bcast, c + 3)
                    dve.tensor_copy(G["F1"][:, bass.ds(c * CHUNK, CHUNK)], f_ps[:, b]).then_inc(f_copied, 1)

        @block.scalar
        def _(act):
            act.wait_ge(u_done, 1)
            act.activation(ub[:], u_ps[:], ACT.Copy).then_inc(ub_ready, 1)
            act.wait_ge(args_ready, 1)
            for out, arg, scale, bias in ((G["A"], s, 1.0, 0.0), (G["Cf"], s_small, 1.0, 0.0),
                                          (G["e1"], f, 1.0, gmax[:, 2:3]), (G["e2"], f, SLOPE, gmax[:, 3:4])):
                act.activation(out[:], arg[:, 1] if arg is f else arg[:], ACT.Exp, scale=scale, bias=bias)
            with act.Fori(0, CHUNKS // 2) as cc:
                for b in range(2):
                    c = 2 * cc + b
                    act.wait_ge(f_bcast, c + 1)
                    for k in range(TPC):
                        last = act.activation(diag[:, b, k * P:(k + 1) * P], G["ident"][:], ACT.Copy,
                                              scale=G["f1"][:, bass.ds(c * TPC + k, 1)])
                    last.then_inc(diag_ready, 1)

        @block.tensor
        def _(pe):
            pe.wait_ge(wrow_ready, 2)
            for i in range(2):
                last = pe.matmul(u_ps[:, i], wrow[:, i], W1[:], start=True, stop=True)
            last.then_inc(u_done, 1)
            pe.sem_inc(f_bcast, 2)
            with pe.Fori(0, CHUNKS // 2) as cc:
                for b in range(2):
                    c = 2 * cc + b
                    pe.wait_ge(diag_ready, c + 1)
                    pe.wait_ge(f_copied, c + 1)
                    pe.matmul(f_ps[:, b], G["ones"][:], diag[:, b], start=True, stop=True).then_inc(f_bcast, 1)


def source_factors(nc, io, G):
    GT = 16
    NG = TILES // GT
    with ExitStack() as ctx:
        sb = lambda n, s, d=F32: ctx.enter_context(nc.sbuf_tensor(n, s, d))
        sem = lambda n: ctx.enter_context(nc.semaphore(n))
        x = sb("x", [P, 2, GT, D])
        full1 = sb("full1", [P, GT, ONE])
        full2 = sb("full2", [P, GT, ONE])
        sum_ps = ctx.enter_context(nc.psum_tensor("sum_ps", [P, D], F32))
        x_in0, x_in1 = sem("x_in0"), sem("x_in1")
        x_in = [x_in0, x_in1]
        x_used, x_summed, full_ready, part_ready, rest_ready, mid_ready, dve_step = (
            sem("x_used"), sem("x_summed"), sem("full_ready"), sem("part_ready"), sem("rest_ready"),
            sem("mid_ready"), sem("dve_step2"))
        block = ctx.enter_context(nc.Block())

        @block.sync
        def _(sp):
            src = io["x"].rearrange("(p g t) f -> g p (t f)", p=P, g=NG)
            for g in range(NG):
                if g >= 2:
                    sp.wait_ge(x_used, g - 1)
                    sp.wait_ge(x_summed, g - 1)
                sp.dma_start(x[:, g % 2].rearrange("p t f -> p (t f)"), src[g]).then_inc(x_in[g % 2], 16)

        @block.tensor
        def _(pe):
            for g in range(NG):
                pe.wait_ge(x_in[g % 2], 16 * (g // 2 + 1))
                for k in range(GT):
                    last = pe.matmul(sum_ps[:], G["ones"][:], x[:, g % 2, k], start=(g == 0 and k == 0),
                                     stop=(g == NG - 1 and k == GT - 1))
                last.then_inc(x_summed, 1)

        @block.vector
        def _(dve):
            for g in range(NG):
                dve.wait_ge(x_in[g % 2], 16 * (g // 2 + 1))
                if g >= 1:
                    dve.wait_ge(part_ready, 2 * g)
                    dve.wait_ge(mid_ready, g)
                tiles = slice(g * GT, (g + 1) * GT)
                for full, e in ((full1, G["e1"]), (full2, G["e2"])):
                    dve.tensor_tensor(full[:, :, 0:D], x[:, g % 2],
                                      bcast(e[:, tiles].unsqueeze(2), [P, GT, D]), ALU.mult
                                      ).then_inc(x_used if full is full2 else dve_step, 1)
                    dve.tensor_copy(full[:, :, D:ONE], e[:, tiles].unsqueeze(2)).then_inc(full_ready, 1)
                dve.wait_ge(part_ready, 2 * g + 1)
                dve.tensor_tensor(full1[:], full1[:], G["XI"][:, tiles, 0], ALU.subtract).then_inc(rest_ready, 1)
                dve.wait_ge(part_ready, 2 * g + 2)
                dve.tensor_tensor(G["XJ"][:, tiles, 1], full2[:], G["XJ"][:, tiles, 0], ALU.subtract
                                  ).then_inc(dve_step, 1)
                dve.wait_ge(mid_ready, g + 1)
                dve.tensor_tensor(G["XI"][:, tiles, 2], full1[:], G["XI"][:, tiles, 1], ALU.subtract
                                  ).then_inc(dve_step, 1)
                dve.wait_ge(dve_step, 3 * (g + 1))
            dve.wait_ge(x_summed, NG)
            dve.tensor_copy(G["SX"][:, 0:D], sum_ps[:])
            dve.memset(G["SX"][:, D:ONE], float(N))

        @block.scalar
        def _(act):
            for g in range(NG):
                tiles = slice(g * GT, (g + 1) * GT)
                act.wait_ge(full_ready, 2 * g + 1)
                act.activation(G["XI"][:, tiles, 0], full1[:], ACT.Copy).then_inc(part_ready, 1)
                act.wait_ge(full_ready, 2 * g + 2)
                act.activation(G["XJ"][:, tiles, 0], full2[:], ACT.Copy).then_inc(part_ready, 1)
                act.wait_ge(rest_ready, g + 1)
                act.activation(G["XI"][:, tiles, 1], full1[:], ACT.Copy).then_inc(mid_ready, 1)


def layer0(nc, io, G):
    NB = 4
    with ExitStack() as ctx:
        sb = lambda n, s, d=F32: ctx.enter_context(nc.sbuf_tensor(n, s, d))
        sem = lambda n: ctx.enter_context(nc.semaphore(n))
        adj = sb("adj", [P, NB, PAIR_W])
        mask = sb("mask", [P, 2, PAIR_W], BF16)
        above = sb("above", [P, 2, PAIR_W], BF16)
        pos = sb("pos", [P, 2, PAIR_W], BF16)
        neg = sb("neg", [P, 2, PAIR_W], BF16)
        xres = sb("xres", [P, TPC, D])
        sums = sb("sums", [P, TPC, 5, ONE])
        total = sb("total", [P, TPC, ONE])
        small = sb("small", [P, 4, TPC])
        stats = sb("stats", [P, TPC, 6])
        mv = sb("mv", [P, TPC, 2])
        acc = ctx.enter_context(nc.psum_tensor("acc0", [P, TPC, 1024], F32))
        adj_in = [sem(f"adj_in{k}") for k in range(NB)]
        mask_made, above_done, pos_done, neg_made, masks_free = (
            sem("mask_made"), sem("above_done"), sem("pos_done"), sem("neg_made"), sem("masks_free"))
        apart = sem("apart0")
        chunk_done, sums_ready, sums_free, xres_in, xres_free, dve_step, var_ready, std_ready, = (sem(n) for n in (
                "chunk_done", "sums_ready", "sums_free", "xres_in", "xres_free", "dve_step3",
                "var_ready", "std_ready"))
        xsrc = io["x"].rearrange("(p t) f -> p t f", p=P)
        block = ctx.enter_context(nc.Block())

        @block.sync
        def _(sp):
            with sp.Fori(0, CHUNKS) as c:
                with sp.Fori(0, PAIRS // NB) as j:
                    turn = c * (PAIRS // NB) + j
                    for k in range(NB):
                        sp.wait_ge(mask_made, turn * NB + k + 1)
                        sp.dma_start(adj[:, k], io["adj"][bass.ds(turn * NB + k, 1)].rearrange("a p w -> (a p) w")
                                     ).then_inc(adj_in[k], 16)

        @block.gpsimd
        def _(pool):
            with pool.Fori(0, CHUNKS) as c:
                pool.wait_ge(xres_free, c + 1)
                pool.dma_start(xres[:], xsrc[:, bass.ds(c * TPC, TPC)]).then_inc(xres_in, 16)

        @block.scalar
        def _(act):
            act.sem_inc(mask_made, NB)
            act.sem_inc(sums_ready, 1)
            with act.Fori(0, CHUNKS) as c:
                with act.Fori(0, PAIRS // NB) as j:
                    turn = c * (PAIRS // NB) + j
                    for k in range(NB):
                        act.wait_ge(adj_in[k], turn * 16 + 16)
                        act.wait_ge(neg_made, turn * NB + k + 1)
                        act.activation(mask[:, k % 2], adj[:, k], ACT.Copy).then_inc(mask_made, 1)
                act.wait_ge(chunk_done, c + 1)
                act.wait_ge(sums_free, c + 1)
                for s in range(TPC):
                    act.activation(sums[:, s, 0:3].rearrange("p a f -> p (a f)"), acc[:, s, 0:3 * ONE], ACT.Copy,
                                   scale=G["A"][:, bass.ds(c * TPC + s, 1)])
                    last = act.activation(sums[:, s, 3:5].rearrange("p a f -> p (a f)"),
                                          acc[:, s, 512:512 + 2 * ONE], ACT.Copy,
                                          scale=G["Cf"][:, bass.ds(c * TPC + s, 1)])
                last.then_inc(sums_ready, 1)
                act.wait_ge(var_ready, c + 1)
                act.activation(small[:, 3], mv[:, :, 1], ACT.Sqrt).then_inc(std_ready, 1)

        @block.vector
        def _(dve):
            dve.sem_inc(neg_made, 2)
            dve.sem_inc(sums_free, 1)
            dve.sem_inc(xres_free, 1)
            with dve.Fori(0, CHUNKS) as c:
                with dve.Fori(0, PAIRS // NB) as j:
                    turn = c * (PAIRS // NB) + j
                    for k in range(NB):
                        b = k % 2
                        load = turn * NB + k
                        for m in range(2):
                            last = dve.tensor_scalar(
                                above[:, b, m * CHUNK:(m + 1) * CHUNK], G["F1"][:, bass.ds(c * CHUNK, CHUNK)],
                                G["neg_f2"][:, bass.ds(j * (2 * NB) + 2 * k + m, 1)], None, ALU.is_gt)
                        last.then_inc(above_done, 1)
                        dve.wait_ge(above_done, load + 1)
                        dve.wait_ge(mask_made, load + 1 + NB)
                        dve.wait_ge(masks_free, load + 1)
                        dve.tensor_tensor(pos[:, b], above[:, b], mask[:, b], ALU.mult).then_inc(pos_done, 1)
                        dve.wait_ge(pos_done, load + 1)
                        dve.tensor_tensor(neg[:, b], mask[:, b], pos[:, b], ALU.subtract).then_inc(neg_made, 1)
                STEPS = 9
                chain = Chain(dve, dve_step, c * STEPS)
                dve.wait_ge(sums_ready, c + 2)
                dve.tensor_tensor(sums[:, :, 2], sums[:, :, 2], sums[:, :, 1], ALU.add)
                chain(dve.tensor_tensor(sums[:, :, 4], sums[:, :, 4], sums[:, :, 3], ALU.add))
                chain(dve.tensor_tensor(sums[:, :, 2], sums[:, :, 2], sums[:, :, 0], ALU.add))
                dve.tensor_tensor(total[:], sums[:, :, 2], sums[:, :, 4], ALU.add).then_inc(sums_free, 1)
                dve.wait_ge(sums_free, c + 2)
                chain(dve.tensor_scalar(small[:, 0], total[:, :, D], 0.0, None, ALU.is_equal))
                for s in range(TPC):
                    last = dve.scalar_tensor_tensor(out=total[:, s], in0=G["SX"][:], scalar=small[:, 0, s:s + 1],
                                                    in1=total[:, s], op0=ALU.mult, op1=ALU.add)
                chain(last)
                chain(dve.reciprocal(small[:, 1], total[:, :, D]))
                dve.wait_ge(xres_in, c * 16 + 16)
                for s in range(TPC):
                    last = dve.scalar_tensor_tensor(out=total[:, s, 0:D], in0=total[:, s, 0:D],
                                                    scalar=small[:, 1, s:s + 1], in1=xres[:, s],
                                                    op0=ALU.mult, op1=ALU.add)
                last.then_inc(xres_free, 1)
                dve.wait_ge(xres_free, c + 2)
                for s in range(TPC):
                    last = dve.bn_stats(stats[:, s], total[:, s, 0:D])
                chain(last)
                dve.sem_inc(apart, 1)
                for s in range(TPC):
                    last = dve.bn_aggr(mv[:, s], stats[:, s])
                chain(last)
                dve.tensor_scalar(mv[:, :, 1], mv[:, :, 1], EPS, None, ALU.add).then_inc(var_ready, 1)
                dve.wait_ge(std_ready, c + 1)
                chain(dve.reciprocal(small[:, 3], small[:, 3]))
                for s in range(TPC):
                    last = dve.tensor_scalar(G["x1"][:, bass.ds(c * TPC + s, 1)].rearrange("p a f -> p (a f)"),
                                             total[:, s, 0:D], mv[:, s, 0:1], small[:, 3, s:s + 1],
                                             ALU.subtract, ALU.mult)
                chain(last)
                assert chain.steps == STEPS

        @block.tensor
        def _(pe):
            pe.sem_inc(masks_free, 2)
            with pe.Fori(0, CHUNKS) as c:
                pe.wait_ge(sums_ready, c + 1)
                for s in range(TPC):
                    for o, w in ((0, 3 * ONE), (512, 2 * ONE)):
                        pe.matmul(acc[:, s, o:o + w], G["zeros"][:, 0:P], G["zeros"][:, 0:w], start=True,
                                  stop=False)
                with pe.Fori(0, PAIRS // NB) as j:
                    turn = c * (PAIRS // NB) + j
                    for k in range(NB):
                        pe.wait_ge(neg_made, turn * NB + k + 3)
                        for m in range(2):
                            t = j * (2 * NB) + 2 * k + m
                            xi = G["XI"][:, bass.ds(t, 1)].rearrange("p a k f -> p (a k f)")
                            xj = G["XJ"][:, bass.ds(t, 1)].rearrange("p a k f -> p (a k f)")
                            for s in range(TPC):
                                w = slice(m * CHUNK + s * P, m * CHUNK + (s + 1) * P)
                                pe.matmul(acc[:, s, 0:3 * ONE], pos[:, k % 2, w], xi, start=False, stop=False)
                                last = pe.matmul(acc[:, s, 512:512 + 2 * ONE], neg[:, k % 2, w], xj,
                                                 start=False, stop=False)
                        last.then_inc(masks_free, 1)
                for s in range(TPC):
                    for o, w in ((0, 3 * ONE), (512, 2 * ONE)):
                        last = pe.matmul(acc[:, s, o:o + w], G["zeros"][:, 0:P], G["zeros"][:, 0:w], start=False,
                                         stop=True)
                last.then_inc(chunk_done, 1)


def projections(nc, io, G):
    with ExitStack() as ctx:
        sb = lambda n, s, d=F32: ctx.enter_context(nc.sbuf_tensor(n, s, d))
        ps = lambda n, s, d=F32: ctx.enter_context(nc.psum_tensor(n, s, d))
        sem = lambda n: ctx.enter_context(nc.semaphore(n))
        xT = sb("xT", [P, 2, CHUNK])
        Wvqk = sb("Wvqk", [P, 3 * D])
        xrow = sb("xrow", [P, 2, TPC, D])
        Wk3 = sb("Wk3", [P, HEADS, 3, C])
        bk3 = sb("bk3", [3 * C, HEADS])
        rows = sb("rows", [P, 3, D])
        prods = sb("prods", [P, 2, 3, D])
        qrow = sb("qrow", [P, 2, D])
        dots = sb("dots", [P, TILES, 3, HEADS])
        guard = sb("guard", [P, HEADS, TILES])
        tmp = sb("tmp", [P, HEADS, TILES])
        root = sb("root", [P, HEADS, TILES])
        kmax = sb("kmax", [P, 2, HEADS])
        shift = sb("shift", [P, CHUNKS, HEADS, TPC])
        shiftT = sb("shiftT", [P, 2, P], FP16)
        xT_ps = ps("xT_ps", [P, 2, CHUNK])
        nat_ps = ps("nat_ps", [P, 2, CHUNK])
        k_ps = ps("k_ps", [P, HEADS, CHUNK])
        (w_in, w_made, xT_made, xT_copied, nat_made, v_taken, q_made, prods_made, kk_made, dots_made, k_made,
         k_high, k_low, xrow_made, ones_row, step, kpart, kall, shift_made, shift_turned, shift_copied, shift_out) = (sem(n) for n in (
             "w_in", "w_made", "xT_made", "xT_copied", "nat_made", "v_taken", "q_made", "prods_made",
             "kk_made", "dots_made", "k_made", "k_high", "k_low", "xrow_made", "ones_row", "pstep", "kpart", "kall", "shift_made",
             "shift_turned", "shift_copied", "shift_out"))
        block = ctx.enter_context(nc.Block())

        @block.sync
        def _(sp):
            for i, k in enumerate(("Wv", "Wq", "Wk")):
                sp.dma_start(Wvqk[:, i * D:(i + 1) * D], io[k]).then_inc(w_in, 16)
            for i, k in enumerate(("bv", "bq", "bk")):
                sp.dma_start(rows[:, i], io[k].partition_broadcast(P)).then_inc(w_in, 16)
            for r in range(3):
                sp.dma_start(bk3[r * C:(r + 1) * C], io["bk_c"]).then_inc(w_in, 16)
            sp.wait_ge(shift_copied, 2)
            sp.dma_start(io["shift"].rearrange("(a p) q -> p a q", a=2), shiftT[:]).then_inc(shift_out, 16)
            sp.wait_ge(shift_out, 16)

        @block.gpsimd
        def _(pool):
            pool.memset(G["Kst"][3 * C:KROWS], 1.0).then_inc(ones_row, 1)
            pool.wait_ge(ones_row, 1)
            pool.wait_ge(kpart, 1)
            pool.partition_all_reduce(kmax[:, 1], kmax[:, 0], P, bass.bass_isa.ReduceOp.max).then_inc(kall, 1)

        @block.tensor
        def _(pe):
            pe.wait_ge(w_made, 1)
            pe.sem_inc(k_made, 2 * HEADS)
            with pe.Fori(0, CHUNKS // 2) as cc:
                for b in range(2):
                    c = 2 * cc + b
                    pe.wait_ge(xrow_made, c + 1)
                    for s in range(TPC):
                        last = pe.transpose(xT_ps[:, b, s * P:(s + 1) * P], xrow[:, b, s], G["ident"][:])
                    last.then_inc(xT_made, 1)
                    pe.wait_ge(xT_copied, c + 1)
                    for s in range(TPC):
                        t = c * TPC + s
                        pe.wait_ge(v_taken, t + 1)
                        pe.wait_ge(kk_made, t + 1)
                        pe.matmul(nat_ps[:, s % 2, 0:3 * D], xT[:, b, s * P:(s + 1) * P], Wvqk[:],
                                  start=True, stop=True).then_inc(nat_made, 1)
                    for h in range(HEADS):
                        pe.wait_ge(k_low, c * HEADS + h + 1)
                        pe.matmul(k_ps[0:3 * C, h], Wk3[:, h].rearrange("p a c -> p (a c)"), xT[:, b],
                                  start=True, stop=True).then_inc(k_made, 1)
            pe.wait_ge(shift_made, 1)
            flat = shift[:].rearrange("p c h s -> p (c h s)")
            for a in range(2):
                pe.transpose(xT_ps[:, a, 0:P], flat[:, a * P:(a + 1) * P], G["ident"][:]).then_inc(shift_turned, 1)

        @block.scalar
        def _(act):
            act.sem_inc(kk_made, 2)
            with act.Fori(0, CHUNKS // 2) as cc:
                for b in range(2):
                    c = 2 * cc + b
                    act.wait_ge(k_made, c * HEADS + HEADS)
                    act.activation(xrow[:, b], G["x1"][:, bass.ds(c * TPC, TPC)], ACT.Copy).then_inc(xrow_made, 1)
                    act.wait_ge(xT_made, c + 1)
                    act.activation(xT[:, b], xT_ps[:, b], ACT.Copy).then_inc(xT_copied, 1)
                    for s in range(TPC):
                        t = c * TPC + s
                        act.wait_ge(v_taken, t + 3)
                        act.wait_ge(dots_made, t + 1)
                        act.activation(prods[:, s % 2, 2], nat_ps[:, s % 2, 2 * D:3 * D], ACT.Square
                                       ).then_inc(kk_made, 1)
                    for h in range(HEADS):
                        act.wait_ge(k_made, c * HEADS + h + 1 + 2 * HEADS)
                        act.activation(G["Kst"][0:3 * C, h, bass.ds(c * CHUNK, CHUNK)], k_ps[0:3 * C, h],
                                       ACT.Identity, bias=bk3[:, h:h + 1]).then_inc(k_high, 1)
            for a in range(2):
                act.wait_ge(shift_turned, a + 1)
                act.activation(shiftT[:, a], xT_ps[:, a, 0:P], ACT.Copy).then_inc(shift_copied, 1)

        @block.vector
        def _(dve):
            chain = Chain(dve, step)
            dve.wait_ge(w_in, 9 * 16)
            for r in range(3):
                last = dve.tensor_copy(Wk3[:, :, r], Wvqk[:, 2 * D:3 * D].rearrange("p (h c) -> p h c", h=HEADS))
            last.then_inc(w_made, 1)
            for start, n in ((v_taken, 2), (dots_made, 2), (k_low, HEADS)):
                dve.sem_inc(start, n)
            with dve.Fori(0, CHUNKS // 2) as cc:
                for half in range(2):
                    c = 2 * cc + half
                    for s in range(TPC):
                        t = c * TPC + s
                        b = s % 2
                        dve.wait_ge(nat_made, t + 1)
                        dve.wait_ge(dots_made, t + 1)
                        dve.tensor_tensor(qrow[:, b], nat_ps[:, b, D:2 * D], rows[:, 1], ALU.add).then_inc(q_made, 1)
                        dve.tensor_tensor(G["v"][:, bass.ds(t, 1)].rearrange("p a f -> p (a f)"),
                                          nat_ps[:, b, 0:D], rows[:, 0], ALU.add).then_inc(v_taken, 1)
                        dve.wait_ge(q_made, t + 1)
                        dve.tensor_tensor(prods[:, b, 0], qrow[:, b], qrow[:, b], ALU.mult)
                        dve.tensor_tensor(prods[:, b, 1], qrow[:, b], rows[:, 2], ALU.mult).then_inc(prods_made, 1)
                        dve.wait_ge(prods_made, t + 1)
                        dve.wait_ge(kk_made, t + 3)
                        dve.tensor_reduce(dots[:, bass.ds(t, 1)].rearrange("p t a h -> p (t a h)"),
                                          prods[:, b].rearrange("p a (h c) -> p (a h) c", h=HEADS), AX.X, ALU.add
                                          ).then_inc(dots_made, 1)
                    for h in range(HEADS):
                        dve.wait_ge(k_high, c * HEADS + h + 1)
                        low = G["Kst"][C:2 * C, h, bass.ds(c * CHUNK, CHUNK)]
                        dve.scalar_tensor_tensor(out=low, in0=k_ps[C:2 * C, h], scalar=bk3[C:2 * C, h:h + 1],
                                                 in1=low, op0=ALU.add, op1=ALU.subtract).then_inc(k_low, 1)
            dve.wait_ge(dots_made, TILES + 2)
            dve.tensor_reduce(kmax[:, 0], dots[:, :, 2].rearrange("p t h -> p h t"), AX.X, ALU.max).then_inc(kpart, 1)
            dve.wait_ge(kall, 1)
            chain(dve.tensor_tensor(guard[:], dots[:, :, 0].rearrange("p t h -> p h t"),
                                    bcast(kmax[:, 1].unsqueeze(2), [P, HEADS, TILES]), ALU.mult))
            rsqrt_newton(chain, dve, root[:], guard[:], tmp[:])
            chain(dve.tensor_tensor(guard[:], guard[:], root[:], ALU.mult))
            chain(dve.tensor_tensor(guard[:], guard[:], dots[:, :, 1].rearrange("p t h -> p h t"), ALU.add))
            dve.tensor_scalar(shift[:].rearrange("p c h s -> p h c s"),
                              guard[:].rearrange("p h (c s) -> p h c s", s=TPC), -1.0, None, ALU.mult
                              ).then_inc(shift_made, 1)




def layer1(nc, io, G):
    NP = 4
    LAG = 3
    LOADS = 2
    HALF = 8
    TURNS = PAIRS // LOADS
    HS = TURNS * HALF
    EPI_STEPS = 15 + RSQRT_STEPS
    with ExitStack() as ctx:
        sb = lambda n, s, d=F32: ctx.enter_context(nc.sbuf_tensor(n, s, d))
        ps = lambda n, s, d=F32: ctx.enter_context(nc.psum_tensor(n, s, d))
        sem = lambda n: ctx.enter_context(nc.semaphore(n))
        adj = sb("adj1", [P, LOADS, 2, CHUNK])
        prob = sb("prob", [P, NP, 2, CHUNK])
        Qst = sb("Qst", [KROWS, 2, HEADS, CHUNK], FP16)
        xrow = sb("xrow1", [P, TPC, D])
        xT = sb("xT1", [P, CHUNK])
        skip = sb("skip", [P, 2, TPC, D])
        stage = sb("stage", [P, 2, HEADS, VW])
        Wq = sb("Wq_", [P, D])
        Wq3 = sb("Wq3", [P, HEADS, 3, C])
        Ws = sb("Ws_", [P, D])
        bq3 = sb("bq3", [3 * C, HEADS])
        bs = sb("bs_", [P, D])
        Wb = sb("Wb_", [P, 3, D])
        outT = sb("outT", [P, 2, CHUNK])
        att = sb("att", [P, TPC, D])
        diff = sb("diff", [P, TPC, D])
        gates = sb("gates", [P, TPC, 3, D])
        den = sb("den", [P, 2, TPC, HEADS])
        z = sb("z", [P, 2, TPC])
        stats = sb("stats1", [P, TPC, 6])
        mv = sb("mv1", [P, TPC, 2])
        rstd = sb("rstd", [P, 3, TPC])
        y = sb("y", [P, TPC, D])
        sc = ps("sc", [P, 2, 2, CHUNK])
        acc = ps("acc1", [P, 2, CHUNK])
        misc = ps("misc", [P, 2, CHUNK])
        adj_in = [sem(f"adj1_in{k}") for k in range(LOADS)]
        apart, pool_apart, y_free = sem("apart1"), sem("pool_apart"), sem("y_free")
        (w_in, w_made, scored, probed, masked, summed, staged, stage_init, acc_done, acc_copied, turned,
         xrow_made, xT_made, xT_copied, q_made, q_high, q_low, skip_summed, skip_made, shift_in, step, att_made,
         z_made, ez_made, y_made, y_out, pool_step) = (sem(n) for n in (
             "w1_in", "w1_made", "scored", "probed", "masked", "summed", "staged", "stage_init", "acc_done",
             "acc_copied", "turned", "xrow1_made", "xT1_made", "xT1_copied", "q1_made", "q_high", "q_low",
             "skip_summed", "skip_made", "shift_in", "step1", "att_made", "z_made", "ez_made", "y_made", "y_out",
             "pool_step1"))
        out_rows = io["out"].rearrange("(p t) f -> p t f", p=P)
        shift_rows = io["shift"].rearrange("(c r) q -> c (r q)", c=CHUNKS)
        block = ctx.enter_context(nc.Block())

        RUNS = [(1, 3), (3, 5), (5, 7), (7, 9), (9, 11), (11, 13), (13, TURNS)]

        def runs(eng, turn_body, pieces):
            for (lo, hi), piece in zip(RUNS, pieces + [()] * (len(RUNS) - len(pieces))):
                with eng.Fori(lo, hi) as j:
                    turn_body(j)
                for part in piece:
                    part()
                if piece and eng is nc.vector:
                    eng.sem_inc(apart, 1)

        @block.sync
        def _(sp):
            for dst, src in ((Wq[:], io["Wq"]), (Ws[:], io["Ws"]), (bs[:], io["bs"].partition_broadcast(P)),
                             (Wb[:].rearrange("p a f -> p (a f)"),
                              io["Wb"].rearrange("a b -> (a b)").partition_broadcast(P))):
                sp.dma_start(dst, src).then_inc(w_in, 16)
            for r in range(3):
                sp.dma_start(bq3[r * C:(r + 1) * C], io["bq_c"]).then_inc(w_in, 16)
            with sp.Fori(0, CHUNKS * TURNS) as turn:
                for k in range(LOADS):
                    sp.wait_ge(masked, turn * HALF + 4 * k + 4)
                    sp.dma_start(adj[:, k].rearrange("p a w -> p (a w)"),
                                 io["adj"][bass.ds(turn * LOADS + k, 1)].rearrange("a p w -> (a p) w")
                                 ).then_inc(adj_in[k], 16)

        @block.gpsimd
        def _(pool):
            pool.memset(stage[:], 0.0).then_inc(pool_step, 1)
            pool.wait_ge(pool_step, 1)
            pool.memset(stage[:, :, :, C:C + 1], 1.0).then_inc(stage_init, 1)
            pool.dma_start(Qst[3 * C:KROWS, 0].rearrange("p h w -> p (h w)"), shift_rows[0:1]).then_inc(shift_in, 16)
            pool.wait_ge(stage_init, 1)
            pool.sem_inc(y_free, 1)

            def stage_values(c, lo, hi):
                with pool.Fori(lo, hi) as j:
                    for b in range(2):
                        wait_apart(pool, summed, (c * TILES + 2 * j + b) * 2 + 2, pool_apart)
                        pool.tensor_copy(stage[:, b, :, 0:C],
                                         G["v"][:, bass.ds(2 * j + b, 1)].rearrange("p a (h c) -> p (a h) c", h=HEADS)
                                         ).then_inc(staged, 1)

            def next_shift(c):
                pool.dma_start(Qst[3 * C:KROWS, bass.ds((c + 1) % 2, 1)].rearrange("p a h w -> p (a h w)"),
                               shift_rows[bass.ds((c + 1) % CHUNKS, 1)]).then_inc(shift_in, 16)

            def store(n):
                pool.wait_ge(y_made, n + 1)
                pool.dma_start(out_rows[:, bass.ds(n * TPC, TPC)], y[:]).then_inc(y_out, 16)

            stage_values(0, 0, 4)
            next_shift(0)
            stage_values(0, 4, TILES // 2)
            with pool.Fori(1, CHUNKS) as c:
                stage_values(c, 0, 4)
                next_shift(c)
                stage_values(c, 4, TILES // 2 - 1)
                store(c - 1)
                stage_values(c, TILES // 2 - 1, TILES // 2)
                pool.wait_ge(y_out, 16 * c)
                pool.sem_inc(y_free, 1)
            store(CHUNKS - 1)
            pool.wait_ge(shift_in, 16 * (CHUNKS + 1))
            pool.wait_ge(y_out, 16 * CHUNKS)

        @block.tensor
        def _(pe):
            def score(c, turn, k):
                pe.wait_ge(probed, c * HS + turn * HALF + k + 1)
                for hh in range(2):
                    h = 2 * (k % 2) + hh
                    last = pe.matmul(sc[:, k % 2, hh], G["Kst"][:, h, bass.ds((turn * (HALF // 2) + k // 2) * P, P)],
                                     Qst[:, bass.ds(c % 2, 1), h].rearrange("p a w -> p (a w)"),
                                     start=True, stop=True)
                last.then_inc(scored, 1)

            def weigh(c, turn, k):
                pe.wait_ge(masked, c * HS + turn * HALF + k + HALF + 1)
                if k % 2 == 0:
                    pe.wait_ge(staged, c * TILES + turn * (HALF // 2) + k // 2 + 1)
                for hh in range(2):
                    last = pe.matmul(acc[hh * VW:(hh + 1) * VW, k % 2], stage[:, (k // 2) % 2, 2 * (k % 2) + hh],
                                     prob[:, k % NP, hh], start=False, stop=False)
                last.then_inc(summed, 1)

            def step_of(c, turn, k):
                score(c, turn, k)
                weigh(c, turn if k >= LAG else turn - 1, (k - LAG) % HALF)

            def edge(c, start):
                for pair in range(2):
                    last = pe.matmul(acc[:, pair], G["zeros"][:, 0:P], G["zeros"][:, 0:CHUNK], start=start,
                                     stop=not start)
                return last

            def turn_source(n):
                pe.wait_ge(xrow_made, n + 1)
                for s in range(TPC):
                    last = pe.transpose(misc[:, 0, s * P:(s + 1) * P], xrow[:, s], G["ident"][:])
                last.then_inc(xT_made, 1)

            def queries(n, heads):
                pe.wait_ge(xT_copied, n + 1)
                for h in heads:
                    if h >= 2:
                        pe.wait_ge(q_low, n * HEADS + h - 1)
                    pe.matmul(misc[0:3 * C, (h + 1) % 2], Wq3[:, h].rearrange("p a c -> p (a c)"), xT[:],
                              start=True, stop=True).then_inc(q_made, 1)

            def skips(n):
                pe.wait_ge(q_low, n * HEADS + HEADS)
                for s in range(TPC):
                    last = pe.matmul(misc[:, 1, s * P:(s + 1) * P], xT[:, s * P:(s + 1) * P], Ws[:],
                                     start=True, stop=True)
                last.then_inc(skip_summed, 1)

            def turn_out(n):
                pe.wait_ge(acc_copied, n + 2)
                for s in range(TPC):
                    for pair in range(2):
                        last = pe.transpose(misc[:, s // 2, (s % 2) * 2 * P + pair * P:(s % 2) * 2 * P + (pair + 1) * P],
                                            outT[:, pair, s * P:(s + 1) * P], G["ident"][:])
                last.then_inc(turned, 1)

            def chunk(c, first):
                pe.wait_ge(q_low, (c + 1) * HEADS)
                pe.wait_ge(shift_in, c * 16 + 16)
                for k in range(LAG):
                    score(c, 0, k)
                pe.wait_ge(acc_copied, c + 1)
                edge(c, True)
                for k in range(LAG, HALF):
                    step_of(c, 0, k)

                def turn_body(j):
                    for k in range(HALF):
                        step_of(c, j, k)

                def after_epilogue():
                    if not first:
                        pe.wait_ge(att_made, c)
                runs(pe, turn_body, [
                    [] if first else [lambda: turn_out(c - 1)],
                    [after_epilogue, lambda: turn_source(c + 1)],
                    [lambda: queries(c + 1, (0, 1))],
                    [lambda: queries(c + 1, (2, 3))],
                    [lambda: skips(c + 1)],
                ])
                for k in range(HALF - LAG, HALF):
                    weigh(c, TURNS - 1, k)
                edge(c, False).then_inc(acc_done, 1)

            pe.sem_inc(summed, 4)
            pe.wait_ge(w_made, 1)
            turn_source(0)
            queries(0, range(HEADS))
            skips(0)
            chunk(0, True)
            with pe.Fori(1, CHUNKS) as c:
                chunk(c, False)
            turn_out(CHUNKS - 1)

        @block.scalar
        def _(act):
            def turn_body(c, j):
                for k in range(HALF):
                    act.wait_ge(scored, c * HS + j * HALF + k + 1)
                    act.activation(prob[:, k % NP].rearrange("p a w -> p (a w)"),
                                   sc[:, k % 2].rearrange("p a w -> p (a w)"), ACT.Exp, scale=SCALE
                                   ).then_inc(probed, 1)

            def copy_source(n):
                act.wait_ge(skip_summed, n + 1)
                act.activation(xrow[:], G["x1"][:, bass.ds((n % CHUNKS) * TPC, TPC)], ACT.Copy).then_inc(xrow_made, 1)

            def copy_turned(n):
                act.wait_ge(xT_made, n + 1)
                act.activation(xT[:], misc[:, 0], ACT.Copy).then_inc(xT_copied, 1)

            def high(n, heads):
                for h in heads:
                    act.wait_ge(q_made, n * HEADS + h + 1)
                    act.activation(Qst[0:3 * C, bass.ds(n % 2, 1), h].rearrange("p a w -> p (a w)"),
                                   misc[0:3 * C, (h + 1) % 2], ACT.Identity, bias=bq3[:, h:h + 1]).then_inc(q_high, 1)

            def gate(n):
                act.wait_ge(z_made, n + 1)
                act.activation(z[:, 1], z[:, 0], ACT.Exp, scale=-1.0).then_inc(ez_made, 1)

            def chunk(c, first):
                turn_body(c, 0)
                runs(act, lambda j: turn_body(c, j), [
                    [lambda: copy_source(c + 1)],
                    [lambda: copy_turned(c + 1)],
                    [lambda: high(c + 1, (0, 1))],
                    [lambda: high(c + 1, (2, 3))],
                    [] if first else [lambda: gate(c - 1)],
                ])
                act.wait_ge(acc_done, c + 1)
                if not first:
                    act.wait_ge(turned, c)
                act.activation(outT[:], acc[:], ACT.Copy).then_inc(acc_copied, 1)

            act.sem_inc(probed, 2)
            act.sem_inc(acc_copied, 1)
            act.wait_ge(w_in, 7 * 16)
            copy_source(0)
            copy_turned(0)
            high(0, range(HEADS))
            chunk(0, True)
            with act.Fori(1, CHUNKS) as c:
                chunk(c, False)
            gate(CHUNKS - 1)

        @block.vector
        def _(dve):
            def turn_body(c, j):
                for k in range(HALF):
                    dve.wait_ge(probed, c * HS + j * HALF + k + 3)
                    if k % 4 == 0:
                        dve.wait_ge(adj_in[k // 4], (c * TURNS + j) * 16 + 16)
                    m = (k // 2) % 2
                    dve.tensor_tensor(prob[:, k % NP], prob[:, k % NP],
                                      bcast(adj[:, k // 4, m:m + 1], [P, 2, CHUNK]), ALU.mult).then_inc(masked, 1)

            def low(n, heads):
                for h in heads:
                    dve.wait_ge(q_high, n * HEADS + h + 1)
                    rest = Qst[2 * C:3 * C, bass.ds(n % 2, 1), h].rearrange("p a w -> p (a w)")
                    dve.scalar_tensor_tensor(out=rest, in0=misc[2 * C:3 * C, (h + 1) % 2],
                                             scalar=bq3[2 * C:3 * C, h:h + 1], in1=rest, op0=ALU.add,
                                             op1=ALU.subtract).then_inc(q_low, 1)

            def skips(n):
                dve.wait_ge(skip_summed, n + 2)
                dve.tensor_tensor(skip[:, bass.ds(n % 2, 1)].rearrange("p a s f -> p (a s) f"),
                                  misc[:, 1].rearrange("p (s f) -> p s f", s=TPC),
                                  bcast(bs[:].unsqueeze(1), [P, TPC, D]), ALU.add).then_inc(skip_made, 1)

            def attention(chain, n):
                dve.wait_ge(turned, n + 1)
                sums = misc[:].rearrange("p b (s h w) -> p (b s h) w", h=HEADS, w=VW)
                chain(dve.tensor_copy(den[:, 0].rearrange("p s h -> p (s h)").unsqueeze(2), sums[:, :, C:C + 1]))
                chain(dve.tensor_scalar(den[:, 1], den[:, 0], 0.0, None, ALU.is_equal))
                chain(dve.tensor_tensor(den[:, 0], den[:, 0], den[:, 1], ALU.add))
                chain(dve.reciprocal(den[:, 1], den[:, 0]))
                dve.tensor_tensor(att[:].rearrange("p s (c h) -> p s h c", h=HEADS),
                                  misc[:].rearrange("p b (s h w) -> p (b s) h w", h=HEADS, w=VW)[:, :, :, 0:C],
                                  bcast(den[:, 1].unsqueeze(3), [P, TPC, HEADS, C]),
                                  ALU.mult).then_inc(att_made, 1)
                dve.wait_ge(att_made, n + 1)

            def gate_terms(chain, n, which):
                if which == 0:
                    dve.wait_ge(skip_made, n + 1)
                    chain(dve.tensor_tensor(diff[:], att[:], skip[:, bass.ds(n % 2, 1)].rearrange("p a s f -> p (a s) f"),
                                            ALU.subtract))
                part = (att[:], skip[:, bass.ds(n % 2, 1)].rearrange("p a s f -> p (a s) f"), diff[:])[which]
                chain(dve.tensor_tensor(gates[:, :, which], part, bcast(Wb[:, which:which + 1], [P, TPC, D]), ALU.mult))

            def gate_sum(chain, n):
                dve.tensor_reduce(z[:, 0], gates[:].rearrange("p s a f -> p s (a f)"), AX.X, ALU.add).then_inc(z_made, 1)

            def mix(chain, n):
                chain(dve.tensor_tensor(att[:], att[:], G["x1"][:, bass.ds(n * TPC, TPC)], ALU.add))
                dve.wait_ge(ez_made, n + 1)
                chain(dve.tensor_scalar(z[:, 1], z[:, 1], -1.0, -1.0, ALU.mult, ALU.add))
                chain(dve.reciprocal(z[:, 0], z[:, 1]))
                for s in range(TPC):
                    last = dve.scalar_tensor_tensor(out=att[:, s], in0=diff[:, s], scalar=z[:, 0, s:s + 1],
                                                    in1=att[:, s], op0=ALU.mult, op1=ALU.add)
                chain(last)

            def statistics(chain, n):
                for s in range(TPC):
                    last = dve.bn_stats(stats[:, s], att[:, s])
                chain(last)
                dve.sem_inc(apart, 1)
                for s in range(TPC):
                    last = dve.bn_aggr(mv[:, s], stats[:, s])
                chain(last)
                chain(dve.tensor_scalar(rstd[:, 0], mv[:, :, 1], EPS, None, ALU.add))
                rsqrt_newton(chain, dve, rstd[:, 1], rstd[:, 0], rstd[:, 2])

            def norm(chain, n):
                dve.wait_ge(y_free, n + 1)
                for s in range(TPC):
                    last = dve.tensor_scalar(y[:, s], att[:, s], mv[:, s, 0:1], rstd[:, 1, s:s + 1],
                                             ALU.subtract, ALU.mult)
                last.then_inc(y_made, 1)

            def chunk(c, first):
                turn_body(c, 0)
                n = c - 1
                chain = Chain(dve, step, None if first else n * EPI_STEPS)
                runs(dve, lambda j: turn_body(c, j), [
                    [] if first else [lambda: attention(chain, n)],
                    [] if first else [lambda: gate_terms(chain, n, 0)],
                    ([] if first else [lambda: gate_terms(chain, n, 1)]) + [lambda: low(c + 1, (0, 1))],
                    ([] if first else [lambda: gate_terms(chain, n, 2), lambda: gate_sum(chain, n)])
                    + [lambda: low(c + 1, (2, 3))],
                    [lambda: skips_after(c + 1)] + ([] if first else [lambda: mix(chain, n)]),
                    [] if first else [lambda: statistics(chain, n)],
                    [] if first else [lambda: norm(chain, n)],
                ])
                assert first or chain.steps == EPI_STEPS, chain.steps

            def skips_after(n):
                skips(n)

            dve.sem_inc(masked, HALF)
            dve.wait_ge(w_in, 7 * 16)
            for r in range(3):
                last = dve.tensor_copy(Wq3[:, :, r], Wq[:].rearrange("p (h c) -> p h c", h=HEADS))
            last.then_inc(w_made, 1)
            dve.sem_inc(skip_summed, 1)
            low(0, range(HEADS))
            skips(0)
            chunk(0, True)
            with dve.Fori(1, CHUNKS) as c:
                chunk(c, False)
            n = CHUNKS - 1
            chain = Chain(dve, step, n * EPI_STEPS)
            attention(chain, n)
            for which in range(3):
                gate_terms(chain, n, which)
            gate_sum(chain, n)
            mix(chain, n)
            statistics(chain, n)
            norm(chain, n)


def program(nc, io):
    with ExitStack() as ctx:
        sb = lambda n, s, d=F32: ctx.enter_context(nc.sbuf_tensor(n, s, d))
        G = {"ident": sb("ident", [P, P]), "ones": sb("ones", [P, P]), "zeros": sb("zeros", [P, CHUNK], BF16),
             "x1": sb("x1", [P, TILES, D])}
        with ExitStack() as first:
            sb0 = lambda n, s, d=F32: first.enter_context(nc.sbuf_tensor(n, s, d))
            for n in ("f1", "neg_f2", "A", "Cf", "e1", "e2"):
                G[n] = sb0(n, [P, TILES])
            G["F1"] = sb0("F1", [P, N])
            G["XI"] = sb0("XI", [P, TILES, 3, ONE], BF16)
            G["XJ"] = sb0("XJ", [P, TILES, 2, ONE], FP16)
            G["SX"] = sb0("SX", [P, ONE])
            node_logits(nc, io, G)
            source_factors(nc, io, G)
            layer0(nc, io, G)
        G["Kst"] = sb("Kst", [KROWS, HEADS, N], FP16)
        G["v"] = sb("v", [P, TILES, D])
        projections(nc, io, G)
        layer1(nc, io, G)


_NAMES = {"x": "x", "inl": "L0_gnn_inlayer2", "W1": "L0_gnn_W1", "w2": "L0_gnn_w2", "w3": "L0_gnn_w3",
          "b2": "L0_gnn_b2", "b3": "L0_gnn_b3", "Wq": "L1_gnn_Wq", "bq": "L1_gnn_bq", "Wk": "L1_gnn_Wk",
          "bk": "L1_gnn_bk", "Wv": "L1_gnn_Wv", "bv": "L1_gnn_bv", "Ws": "L1_gnn_Ws", "bs": "L1_gnn_bs",
          "Wb": "L1_gnn_Wb"}


def kernel(**inputs):
    import numpy as np
    import concourse.bacc as bacc
    from concourse.bass_utils import run_bass_kernel_spmd

    arrays = {k: np.asarray(inputs[name]) for k, name in _NAMES.items()}
    for k in ("b2", "b3"):
        arrays[k] = arrays[k].reshape(1, 1)
    for k in ("bq", "bk"):
        arrays[k + "_c"] = arrays[k].reshape(HEADS, C).T
    adj = np.asarray(inputs["adj"]).reshape(P, CHUNKS, TPC, P, PAIRS, 2)
    arrays["adj"] = adj.transpose(1, 4, 3, 5, 2, 0).reshape(CHUNKS * PAIRS, P, PAIR_W)
    nc = bacc.Bacc("TRN2", target_bir_lowering=False, num_devices=1)
    io, sent = {}, {}
    for k, a in arrays.items():
        sent[f"in_{k}_dram"] = np.ascontiguousarray(a)
        io[k] = nc.dram_tensor(f"in_{k}_dram", a.shape, mybir.dt.from_np(a.dtype), kind="ExternalInput").ap()
    io["out"] = nc.dram_tensor("out_dram", (N, D), F32, kind="ExternalOutput").ap()
    io["shift"] = nc.dram_tensor("shift_dram", (CHUNKS * HEADS * TPC, P), FP16, kind="Internal").ap()
    program(nc, io)
    return run_bass_kernel_spmd(nc, [sent], core_ids=[0]).results[0]["out_dram"]
```

```python
from contextlib import ExitStack

import concourse.bass as bass
import concourse.mybir as mybir
from concourse.alu_op_type import AluOpType as ALU

F32 = mybir.dt.float32
BF16 = mybir.dt.bfloat16
FP16 = mybir.dt.float16
I32 = mybir.dt.int32
ACT = mybir.ActivationFunctionType
AX = mybir.AxisListType

P = 128
N = 8192
D = 128
HEADS = 4
C = D // HEADS
TILES = N // P
TPC = 4
CHUNK = TPC * P
CHUNKS = N // CHUNK
PAIRS = TILES // 2
PAIR_W = 2 * CHUNK
ONE = D + 1
SLOPE = 0.01
EPS = 1e-5
SCALE = float(C) ** -0.5
RSQRT_MAGIC = 1597463007.0
VW = 64
KROWS = 3 * C + 1


class Chain:

    def __init__(self, eng, sem, start=0):
        self.eng, self.sem, self.n = eng, sem, start
        self.steps = 0

    def __call__(self, ins):
        ins.then_inc(self.sem, 1)
        self.n = self.n + 1
        self.steps += 1
        self.eng.wait_ge(self.sem, self.n)


def wait_apart(eng, sem, value, mark):
    eng.wait_ge(sem, value)
    eng.sem_inc(mark, 1)


def bcast(ap, shape):
    return ap.to_broadcast(shape)


def rsqrt_newton(chain, dve, out, v, tmp):
    chain(dve.tensor_scalar(out.bitcast(I32), v.bitcast(I32), -0.5, RSQRT_MAGIC, ALU.mult, ALU.add))
    for _ in range(4):
        chain(dve.tensor_tensor(tmp, out, out, ALU.mult))
        chain(dve.tensor_tensor(tmp, tmp, v, ALU.mult))
        chain(dve.tensor_scalar(tmp, tmp, -0.5, 1.5, ALU.mult, ALU.add))
        chain(dve.tensor_tensor(out, out, tmp, ALU.mult))


RSQRT_STEPS = 17


def node_logits(nc, io, G):
    GT = 8
    NG = TILES // GT
    with ExitStack() as ctx:
        sb = lambda n, s, d=F32: ctx.enter_context(nc.sbuf_tensor(n, s, d))
        ps = lambda n, s, d=F32: ctx.enter_context(nc.psum_tensor(n, s, d))
        sem = lambda n: ctx.enter_context(nc.semaphore(n))
        inl = sb("inl", [P, 2, GT, 2 * D])
        junk = sb("junk", [P, 4, 2 * D])
        W1 = sb("W1", [P, 2 * D])
        wcol = sb("wcol", [P, 2])
        bcol = sb("bcol", [P, 2])
        wrow = sb("wrow", [P, 2, P])
        ub = sb("ub", [P, 2, 2 * D])
        f = sb("f", [P, 2, TILES])
        s = sb("s", [P, TILES])
        s_small = sb("s_small", [P, TILES])
        s_max = sb("s_max", [P, TILES])
        gmax = sb("gmax", [P, 4])
        diag = sb("diag", [P, 2, CHUNK])
        u_ps = ps("u_ps", [P, 2, 2 * D])
        f_ps = ps("f_ps", [P, 2, CHUNK])
        weights_in, inl_in0, inl_in1 = sem("weights_in"), sem("inl_in0"), sem("inl_in1")
        inl_in = [inl_in0, inl_in1]
        dots_done, consts_ready, wrow_ready, u_done, ub_ready = (
            sem("dots_done"), sem("consts_ready"), sem("wrow_ready"), sem("u_done"), sem("ub_ready"))
        dve_step, act_step, pool_step = sem("dve_step"), sem("act_step"), sem("pool_step")
        f_ready, gpart_ready, gmax_ready, args_ready = (
            sem("f_ready"), sem("gpart_ready"), sem("gmax_ready"), sem("args_ready"))
        diag_ready, f_bcast, f_copied = sem("diag_ready"), sem("f_bcast"), sem("f_copied")
        block = ctx.enter_context(nc.Block())

        @block.sync
        def _(sp):
            sp.dma_start(W1[:], io["W1"]).then_inc(weights_in, 16)
            for i, k in enumerate(("w2", "w3")):
                sp.dma_start(wcol[:, i:i + 1], io[k].rearrange("(p a) -> p a", a=1)).then_inc(weights_in, 16)
            for i, k in enumerate(("b2", "b3")):
                sp.dma_start(bcol[:, i:i + 1], io[k].partition_broadcast(P).rearrange("p a b -> p (a b)")
                             ).then_inc(weights_in, 16)
            src = io["inl"].rearrange("(p g t) f -> g p (t f)", p=P, g=NG)
            with sp.Fori(0, NG // 2) as gg:
                for b in range(2):
                    sp.wait_ge(dots_done, (2 * gg + b) * (2 * GT) + 2 * GT)
                    sp.dma_start(inl[:, b].rearrange("p t f -> p (t f)"),
                                 src[bass.ds(2 * gg + b, 1)].rearrange("a p w -> (a p) w")).then_inc(inl_in[b], 16)

        @block.gpsimd
        def _(pool):
            chain = Chain(pool, pool_step)
            chain(pool.memset(G["ident"][:], 0.0))
            pool.affine_select(out=G["ident"][:], in_=G["ident"][:], compare_op=ALU.not_equal, fill=1.0,
                               base=0, pattern=[[-1, P]], channel_multiplier=1).then_inc(consts_ready, 1)
            pool.memset(G["ones"][:], 1.0).then_inc(consts_ready, 1)
            pool.memset(G["zeros"][:], 0.0).then_inc(consts_ready, 1)
            pool.wait_ge(gpart_ready, 1)
            pool.partition_all_reduce(gmax[:, 1:2], gmax[:, 0:1], P, bass.bass_isa.ReduceOp.max
                                      ).then_inc(gmax_ready, 1)

        @block.vector
        def _(dve):
            chain = Chain(dve, dve_step)
            dve.wait_ge(weights_in, 5 * 16)
            dve.wait_ge(consts_ready, 3)
            for i in range(2):
                dve.tensor_scalar(wrow[:, i], G["ones"][:], wcol[:, i:i + 1], None, ALU.mult
                                  ).then_inc(wrow_ready, 1)
            dve.sem_inc(dots_done, 4 * GT)
            dve.wait_ge(ub_ready, 1)
            with dve.Fori(0, NG // 2) as gg:
                for b in range(2):
                    dve.wait_ge(inl_in[b], gg * 16 + 16)
                    for k in range(2 * GT):
                        t, i = k // 2, k % 2
                        dve.wait_ge(dots_done, (2 * gg + b) * (2 * GT) + k + 4 * GT - 3)
                        dve.scalar_tensor_tensor(
                            out=junk[:, k % 4], in0=inl[:, b, t], scalar=1.0, in1=ub[:, i], op0=ALU.mult,
                            op1=ALU.mult, accum_out=f[:, i, bass.ds((2 * gg + b) * GT + t, 1)]
                        ).then_inc(dots_done, 1)
            dve.wait_ge(dots_done, 2 * TILES + 4 * GT)
            dve.tensor_scalar(G["f1"][:], f[:, 0], bcol[:, 0:1], None, ALU.add).then_inc(f_ready, 1)
            chain(dve.tensor_scalar(f[:, 1], f[:, 1], bcol[:, 1:2], None, ALU.add))
            dve.reduce_max(gmax[:, 0:1], f[:, 1], AX.X).then_inc(gpart_ready, 1)
            dve.tensor_scalar(G["neg_f2"][:], f[:, 1], -1.0, None, ALU.mult)
            dve.wait_ge(gmax_ready, 1)
            dve.wait_ge(f_ready, 1)
            chain(dve.tensor_scalar(s[:], G["f1"][:], gmax[:, 1:2], None, ALU.add))
            chain(dve.tensor_scalar(s_small[:], s[:], SLOPE, None, ALU.mult))
            chain(dve.tensor_tensor(s_max[:], s[:], s_small[:], ALU.max))
            chain(dve.tensor_tensor(s[:], s[:], s_max[:], ALU.subtract))
            chain(dve.tensor_tensor(s_small[:], s_small[:], s_max[:], ALU.subtract))
            chain(dve.tensor_scalar(gmax[:, 2:3], gmax[:, 1:2], -1.0, None, ALU.mult))
            dve.tensor_scalar(gmax[:, 3:4], gmax[:, 1:2], -SLOPE, None, ALU.mult).then_inc(args_ready, 1)
            dve.sem_inc(f_copied, 2)
            with dve.Fori(0, CHUNKS // 2) as cc:
                for b in range(2):
                    c = 2 * cc + b
                    dve.wait_ge(f_bcast, c + 3)
                    dve.tensor_copy(G["F1"][:, bass.ds(c * CHUNK, CHUNK)], f_ps[:, b]).then_inc(f_copied, 1)

        @block.scalar
        def _(act):
            act.wait_ge(u_done, 1)
            act.activation(ub[:], u_ps[:], ACT.Copy).then_inc(ub_ready, 1)
            act.wait_ge(args_ready, 1)
            for out, arg, scale, bias in ((G["A"], s, 1.0, 0.0), (G["Cf"], s_small, 1.0, 0.0),
                                          (G["e1"], f, 1.0, gmax[:, 2:3]), (G["e2"], f, SLOPE, gmax[:, 3:4])):
                act.activation(out[:], arg[:, 1] if arg is f else arg[:], ACT.Exp, scale=scale, bias=bias)
            with act.Fori(0, CHUNKS // 2) as cc:
                for b in range(2):
                    c = 2 * cc + b
                    act.wait_ge(f_bcast, c + 1)
                    for k in range(TPC):
                        last = act.activation(diag[:, b, k * P:(k + 1) * P], G["ident"][:], ACT.Copy,
                                              scale=G["f1"][:, bass.ds(c * TPC + k, 1)])
                    last.then_inc(diag_ready, 1)

        @block.tensor
        def _(pe):
            pe.wait_ge(wrow_ready, 2)
            for i in range(2):
                last = pe.matmul(u_ps[:, i], wrow[:, i], W1[:], start=True, stop=True)
            last.then_inc(u_done, 1)
            pe.sem_inc(f_bcast, 2)
            with pe.Fori(0, CHUNKS // 2) as cc:
                for b in range(2):
                    c = 2 * cc + b
                    pe.wait_ge(diag_ready, c + 1)
                    pe.wait_ge(f_copied, c + 1)
                    pe.matmul(f_ps[:, b], G["ones"][:], diag[:, b], start=True, stop=True).then_inc(f_bcast, 1)


def source_factors(nc, io, G):
    GT = 16
    NG = TILES // GT
    with ExitStack() as ctx:
        sb = lambda n, s, d=F32: ctx.enter_context(nc.sbuf_tensor(n, s, d))
        sem = lambda n: ctx.enter_context(nc.semaphore(n))
        x = sb("x", [P, 2, GT, D])
        full1 = sb("full1", [P, GT, ONE])
        full2 = sb("full2", [P, GT, ONE])
        sum_ps = ctx.enter_context(nc.psum_tensor("sum_ps", [P, D], F32))
        x_in0, x_in1 = sem("x_in0"), sem("x_in1")
        x_in = [x_in0, x_in1]
        x_used, x_summed, full_ready, part_ready, rest_ready, mid_ready, dve_step = (
            sem("x_used"), sem("x_summed"), sem("full_ready"), sem("part_ready"), sem("rest_ready"),
            sem("mid_ready"), sem("dve_step2"))
        block = ctx.enter_context(nc.Block())

        @block.sync
        def _(sp):
            src = io["x"].rearrange("(p g t) f -> g p (t f)", p=P, g=NG)
            for g in range(NG):
                if g >= 2:
                    sp.wait_ge(x_used, g - 1)
                    sp.wait_ge(x_summed, g - 1)
                sp.dma_start(x[:, g % 2].rearrange("p t f -> p (t f)"), src[g]).then_inc(x_in[g % 2], 16)

        @block.tensor
        def _(pe):
            for g in range(NG):
                pe.wait_ge(x_in[g % 2], 16 * (g // 2 + 1))
                for k in range(GT):
                    last = pe.matmul(sum_ps[:], G["ones"][:], x[:, g % 2, k], start=(g == 0 and k == 0),
                                     stop=(g == NG - 1 and k == GT - 1))
                last.then_inc(x_summed, 1)

        @block.vector
        def _(dve):
            for g in range(NG):
                dve.wait_ge(x_in[g % 2], 16 * (g // 2 + 1))
                if g >= 1:
                    dve.wait_ge(part_ready, 2 * g)
                    dve.wait_ge(mid_ready, g)
                tiles = slice(g * GT, (g + 1) * GT)
                for full, e in ((full1, G["e1"]), (full2, G["e2"])):
                    dve.tensor_tensor(full[:, :, 0:D], x[:, g % 2],
                                      bcast(e[:, tiles].unsqueeze(2), [P, GT, D]), ALU.mult
                                      ).then_inc(x_used if full is full2 else dve_step, 1)
                    dve.tensor_copy(full[:, :, D:ONE], e[:, tiles].unsqueeze(2)).then_inc(full_ready, 1)
                dve.wait_ge(part_ready, 2 * g + 1)
                dve.tensor_tensor(full1[:], full1[:], G["XI"][:, tiles, 0], ALU.subtract).then_inc(rest_ready, 1)
                dve.wait_ge(part_ready, 2 * g + 2)
                dve.tensor_tensor(G["XJ"][:, tiles, 1], full2[:], G["XJ"][:, tiles, 0], ALU.subtract
                                  ).then_inc(dve_step, 1)
                dve.wait_ge(mid_ready, g + 1)
                dve.tensor_tensor(G["XI"][:, tiles, 2], full1[:], G["XI"][:, tiles, 1], ALU.subtract
                                  ).then_inc(dve_step, 1)
                dve.wait_ge(dve_step, 3 * (g + 1))
            dve.wait_ge(x_summed, NG)
            dve.tensor_copy(G["SX"][:, 0:D], sum_ps[:])
            dve.memset(G["SX"][:, D:ONE], float(N))

        @block.scalar
        def _(act):
            for g in range(NG):
                tiles = slice(g * GT, (g + 1) * GT)
                act.wait_ge(full_ready, 2 * g + 1)
                act.activation(G["XI"][:, tiles, 0], full1[:], ACT.Copy).then_inc(part_ready, 1)
                act.wait_ge(full_ready, 2 * g + 2)
                act.activation(G["XJ"][:, tiles, 0], full2[:], ACT.Copy).then_inc(part_ready, 1)
                act.wait_ge(rest_ready, g + 1)
                act.activation(G["XI"][:, tiles, 1], full1[:], ACT.Copy).then_inc(mid_ready, 1)


def layer0(nc, io, G):
    NB = 4
    TURNS = PAIRS // NB
    with ExitStack() as ctx:
        sb = lambda n, s, d=F32: ctx.enter_context(nc.sbuf_tensor(n, s, d))
        sem = lambda n: ctx.enter_context(nc.semaphore(n))
        adj = sb("adj", [P, NB, PAIR_W])
        mask = sb("mask", [P, NB, PAIR_W], BF16)
        pos = sb("pos", [P, NB, PAIR_W], BF16)
        neg = sb("neg", [P, NB, PAIR_W], BF16)
        xres = sb("xres", [P, TPC, D])
        sums = sb("sums", [P, TPC, 5, ONE])
        small = sb("small", [P, 2, TPC])
        stats = sb("stats", [P, TPC, 6])
        mv = sb("mv", [P, TPC, 2])
        mvs = sb("mvs", [P, TILES, 2])
        rstd = sb("rstd0", [P, 3, TILES])
        acc = ctx.enter_context(nc.psum_tensor("acc0", [P, TPC, 1024], F32))
        adj_in = [sem(f"adj_in{k}") for k in range(NB)]
        mask_made, pos_done, neg_made, masks_free = (
            sem("mask_made"), sem("pos_done"), sem("neg_made"), sem("masks_free"))
        apart = sem("apart0")
        summed, banks_free, sums_free, xres_in, xres_free, dve_step, normed = (sem(n) for n in (
            "summed0", "banks_free", "sums_free", "xres_in", "xres_free", "dve_step3", "normed"))
        xsrc = io["x"].rearrange("(p t) f -> p t f", p=P)
        block = ctx.enter_context(nc.Block())

        RUNS = [(0, 2), (2, 3), (3, 4), (4, 5), (5, 6), (6, TURNS)]

        @block.sync
        def _(sp):
            with sp.Fori(0, CHUNKS * TURNS) as turn:
                for k in range(NB):
                    sp.wait_ge(mask_made, turn * NB + k + 1)
                    sp.dma_start(adj[:, k], io["adj"][bass.ds(turn * NB + k, 1)].rearrange("a p w -> (a p) w")
                                 ).then_inc(adj_in[k], 16)

        @block.gpsimd
        def _(pool):
            with pool.Fori(0, CHUNKS) as c:
                pool.wait_ge(xres_free, c + 1)
                pool.dma_start(xres[:], xsrc[:, bass.ds(c * TPC, TPC)]).then_inc(xres_in, 16)

        @block.scalar
        def _(act):
            def turn_body(turn):
                for k in range(NB):
                    act.wait_ge(adj_in[k], turn * 16 + 16)
                    act.wait_ge(neg_made, turn * NB + k + 1)
                    act.activation(mask[:, k], adj[:, k], ACT.Copy).then_inc(mask_made, 1)

            def evacuate(n):
                act.wait_ge(sums_free, n + 1)
                for s in range(TPC):
                    act.wait_ge(summed, n * TPC + s + 1)
                    part = act.activation(sums[:, s, 0:3].rearrange("p a f -> p (a f)"), acc[:, s, 0:3 * ONE],
                                          ACT.Copy, scale=G["A"][:, bass.ds(n * TPC + s, 1)])
                    if s == TPC - 1:
                        part.then_inc(masks_free, 1)
                    act.activation(sums[:, s, 3:5].rearrange("p a f -> p (a f)"),
                                   acc[:, s, 512:512 + 2 * ONE], ACT.Copy,
                                   scale=G["Cf"][:, bass.ds(n * TPC + s, 1)]).then_inc(banks_free, 1)

            act.sem_inc(mask_made, NB)
            act.sem_inc(banks_free, TPC)
            with act.Fori(0, TURNS) as turn:
                turn_body(turn)
            with act.Fori(1, CHUNKS) as c:
                turn_body(c * TURNS)
                evacuate(c - 1)
                with act.Fori(1, TURNS) as j:
                    turn_body(c * TURNS + j)
            evacuate(CHUNKS - 1)

        @block.vector
        def _(dve):
            def make_pos(c, j, k):
                dve.wait_ge(mask_made, (c * TURNS + j) * NB + k + 1 + NB)
                dve.wait_ge(masks_free, (c * TURNS + j) * NB + k + 1)
                for m in range(2):
                    w = slice(m * CHUNK, (m + 1) * CHUNK)
                    last = dve.scalar_tensor_tensor(
                        out=pos[:, k, w], in0=G["F1"][:, bass.ds(c * CHUNK, CHUNK)],
                        scalar=G["neg_f2"][:, bass.ds(j * (2 * NB) + 2 * k + m, 1)], in1=mask[:, k, w],
                        op0=ALU.is_gt, op1=ALU.mult)
                last.then_inc(pos_done, 1)

            def make_neg(c, j, k):
                dve.wait_ge(pos_done, (c * TURNS + j) * NB + k + 1)
                dve.tensor_tensor(neg[:, k], mask[:, k], pos[:, k], ALU.subtract).then_inc(neg_made, 1)

            def turn_body(c, j):
                make_pos(c, j, 0)
                for k in range(1, NB):
                    make_pos(c, j, k)
                    make_neg(c, j, k - 1)
                make_neg(c, j, NB - 1)

            def add_parts(chain, n):
                dve.wait_ge(banks_free, (n + 2) * TPC)
                dve.tensor_tensor(sums[:, :, 2], sums[:, :, 2], sums[:, :, 1], ALU.add)
                chain(dve.tensor_tensor(sums[:, :, 4], sums[:, :, 4], sums[:, :, 3], ALU.add))
                chain(dve.tensor_tensor(sums[:, :, 2], sums[:, :, 2], sums[:, :, 0], ALU.add))

            def add_sides(chain, n):
                chain(dve.tensor_tensor(sums[:, :, 2], sums[:, :, 2], sums[:, :, 4], ALU.add))
                chain(dve.tensor_scalar(small[:, 0], sums[:, :, 2, D], 0.0, None, ALU.is_equal))
                for s in range(TPC):
                    last = dve.scalar_tensor_tensor(out=sums[:, s, 2], in0=G["SX"][:], scalar=small[:, 0, s:s + 1],
                                                    in1=sums[:, s, 2], op0=ALU.mult, op1=ALU.add)
                chain(last)

            def residual(chain, n):
                chain(dve.reciprocal(small[:, 1], sums[:, :, 2, D]))
                dve.wait_ge(xres_in, n * 16 + 16)
                for s in range(TPC):
                    last = dve.scalar_tensor_tensor(
                        out=G["x1"][:, bass.ds(n * TPC + s, 1)].rearrange("p a f -> p (a f)"),
                        in0=sums[:, s, 2, 0:D], scalar=small[:, 1, s:s + 1], in1=xres[:, s],
                        op0=ALU.mult, op1=ALU.add)
                last.then_inc(xres_free, 1)
                dve.wait_ge(xres_free, n + 2)
                dve.sem_inc(sums_free, 1)

            def statistics(chain, n):
                for s in range(TPC):
                    last = dve.bn_stats(stats[:, s], G["x1"][:, bass.ds(n * TPC + s, 1)].rearrange("p a f -> p (a f)"))
                chain(last)
                dve.sem_inc(apart, 1)
                for s in range(TPC):
                    last = dve.bn_aggr(mv[:, s], stats[:, s])
                chain(last)
                chain(dve.tensor_copy(mvs[:, bass.ds(n * TPC, TPC)], mv[:]))

            PIECES = [add_parts, add_sides, residual, statistics]
            STEPS = 9

            dve.sem_inc(neg_made, NB)
            dve.sem_inc(sums_free, 1)
            dve.sem_inc(xres_free, 1)
            with dve.Fori(0, TURNS) as j:
                turn_body(0, j)
            with dve.Fori(1, CHUNKS) as c:
                chain = Chain(dve, dve_step, (c - 1) * STEPS)
                for i, (lo, hi) in enumerate(RUNS):
                    with dve.Fori(lo, hi) as j:
                        turn_body(c, j)
                    if i < len(PIECES):
                        PIECES[i](chain, c - 1)
                        dve.sem_inc(apart, 1)
                assert chain.steps == STEPS
            n = CHUNKS - 1
            chain = Chain(dve, dve_step, n * STEPS)
            for piece in PIECES:
                piece(chain, n)
            chain(dve.tensor_scalar(rstd[:, 0], mvs[:, :, 1], EPS, None, ALU.add))
            rsqrt_newton(chain, dve, rstd[:, 1], rstd[:, 0], rstd[:, 2])
            dve.sem_inc(apart, 1)
            with dve.Fori(0, CHUNKS) as c:
                for s in range(TPC):
                    row = G["x1"][:, bass.ds(c * TPC + s, 1)].rearrange("p a f -> p (a f)")
                    last = dve.tensor_scalar(
                        row, row, mvs[:, bass.ds(c * TPC + s, 1), 0], rstd[:, 1, bass.ds(c * TPC + s, 1)],
                        ALU.subtract, ALU.mult)
                last.then_inc(normed, 1)
            dve.wait_ge(normed, CHUNKS)

        @block.tensor
        def _(pe):
            def multiply(k, m, s, t, start, stop):
                w = slice(m * CHUNK + s * P, m * CHUNK + (s + 1) * P)
                xi = G["XI"][:, bass.ds(t, 1)].rearrange("p a k f -> p (a k f)")
                xj = G["XJ"][:, bass.ds(t, 1)].rearrange("p a k f -> p (a k f)")
                pe.matmul(acc[:, s, 0:3 * ONE], pos[:, k, w], xi, start=start, stop=stop)
                return pe.matmul(acc[:, s, 512:512 + 2 * ONE], neg[:, k, w], xj, start=start, stop=stop)

            def load(c, j, k):
                pe.wait_ge(neg_made, (c * TURNS + j) * NB + k + 1 + NB)
                for m in range(2):
                    for s in range(TPC):
                        last = multiply(k, m, s, j * (2 * NB) + 2 * k + m, False, False)
                last.then_inc(masks_free, 1)

            pe.sem_inc(masks_free, NB)
            with pe.Fori(0, CHUNKS) as c:
                pe.wait_ge(neg_made, c * TURNS * NB + 1 + NB)
                for s in range(TPC):
                    pe.wait_ge(banks_free, c * TPC + s + 1)
                    for m in range(2):
                        last = multiply(0, m, s, m, m == 0, False)
                last.then_inc(masks_free, 1)
                for k in range(1, NB):
                    load(c, 0, k)
                with pe.Fori(1, TURNS - 1) as j:
                    for k in range(NB):
                        load(c, j, k)
                for k in range(NB - 1):
                    load(c, TURNS - 1, k)
                pe.wait_ge(neg_made, (c * TURNS + TURNS) * NB + NB)
                for s in range(TPC):
                    for m in range(2):
                        last = multiply(NB - 1, m, s, TILES - 2 + m, False, m == 1)
                    last.then_inc(summed, 1)


def projections(nc, io, G):
    with ExitStack() as ctx:
        sb = lambda n, s, d=F32: ctx.enter_context(nc.sbuf_tensor(n, s, d))
        ps = lambda n, s, d=F32: ctx.enter_context(nc.psum_tensor(n, s, d))
        sem = lambda n: ctx.enter_context(nc.semaphore(n))
        xT = sb("xT", [P, 2, CHUNK])
        Wvqk = sb("Wvqk", [P, 3 * D])
        xrow = sb("xrow", [P, 2, TPC, D])
        Wk3 = sb("Wk3", [P, HEADS, 3, C])
        bk3 = sb("bk3", [3 * C, HEADS])
        rows = sb("rows", [P, 3, D])
        prods = sb("prods", [P, 2, 3, D])
        qrow = sb("qrow", [P, 2, D])
        dots = sb("dots", [P, TILES, 3, HEADS])
        guard = sb("guard", [P, HEADS, TILES])
        tmp = sb("tmp", [P, HEADS, TILES])
        root = sb("root", [P, HEADS, TILES])
        kmax = sb("kmax", [P, 2, HEADS])
        shift = sb("shift", [P, CHUNKS, HEADS, TPC])
        shiftT = sb("shiftT", [P, 2, P], FP16)
        xT_ps = ps("xT_ps", [P, 2, CHUNK])
        nat_ps = ps("nat_ps", [P, 2, CHUNK])
        k_ps = ps("k_ps", [P, HEADS, CHUNK])
        (w_in, w_made, xT_made, xT_copied, nat_made, v_taken, q_made, prods_made, kk_made, dots_made, k_made,
         k_high, k_low, xrow_made, ones_row, step, kpart, kall, shift_made, shift_turned, shift_copied, shift_out) = (sem(n) for n in (
             "w_in", "w_made", "xT_made", "xT_copied", "nat_made", "v_taken", "q_made", "prods_made",
             "kk_made", "dots_made", "k_made", "k_high", "k_low", "xrow_made", "ones_row", "pstep", "kpart", "kall", "shift_made",
             "shift_turned", "shift_copied", "shift_out"))
        block = ctx.enter_context(nc.Block())

        @block.sync
        def _(sp):
            for i, k in enumerate(("Wv", "Wq", "Wk")):
                sp.dma_start(Wvqk[:, i * D:(i + 1) * D], io[k]).then_inc(w_in, 16)
            for i, k in enumerate(("bv", "bq", "bk")):
                sp.dma_start(rows[:, i], io[k].partition_broadcast(P)).then_inc(w_in, 16)
            for r in range(3):
                sp.dma_start(bk3[r * C:(r + 1) * C], io["bk_c"]).then_inc(w_in, 16)
            sp.wait_ge(shift_copied, 2)
            sp.dma_start(io["shift"].rearrange("(a p) q -> p a q", a=2), shiftT[:]).then_inc(shift_out, 16)
            sp.wait_ge(shift_out, 16)

        @block.gpsimd
        def _(pool):
            pool.memset(G["Kst"][3 * C:KROWS], 1.0).then_inc(ones_row, 1)
            pool.wait_ge(ones_row, 1)
            pool.wait_ge(kpart, 1)
            pool.partition_all_reduce(kmax[:, 1], kmax[:, 0], P, bass.bass_isa.ReduceOp.max).then_inc(kall, 1)

        @block.tensor
        def _(pe):
            pe.wait_ge(w_made, 1)
            pe.sem_inc(k_made, 2 * HEADS)
            with pe.Fori(0, CHUNKS // 2) as cc:
                for b in range(2):
                    c = 2 * cc + b
                    pe.wait_ge(xrow_made, c + 1)
                    for s in range(TPC):
                        last = pe.transpose(xT_ps[:, b, s * P:(s + 1) * P], xrow[:, b, s], G["ident"][:])
                    last.then_inc(xT_made, 1)
                    pe.wait_ge(xT_copied, c + 1)
                    for s in range(TPC):
                        t = c * TPC + s
                        pe.wait_ge(v_taken, t + 1)
                        pe.wait_ge(kk_made, t + 1)
                        pe.matmul(nat_ps[:, s % 2, 0:3 * D], xT[:, b, s * P:(s + 1) * P], Wvqk[:],
                                  start=True, stop=True).then_inc(nat_made, 1)
                    for h in range(HEADS):
                        pe.wait_ge(k_low, c * HEADS + h + 1)
                        pe.matmul(k_ps[0:3 * C, h], Wk3[:, h].rearrange("p a c -> p (a c)"), xT[:, b],
                                  start=True, stop=True).then_inc(k_made, 1)
            pe.wait_ge(shift_made, 1)
            flat = shift[:].rearrange("p c h s -> p (c h s)")
            for a in range(2):
                pe.transpose(xT_ps[:, a, 0:P], flat[:, a * P:(a + 1) * P], G["ident"][:]).then_inc(shift_turned, 1)

        @block.scalar
        def _(act):
            act.sem_inc(kk_made, 2)
            with act.Fori(0, CHUNKS // 2) as cc:
                for b in range(2):
                    c = 2 * cc + b
                    act.wait_ge(k_made, c * HEADS + HEADS)
                    act.activation(xrow[:, b], G["x1"][:, bass.ds(c * TPC, TPC)], ACT.Copy).then_inc(xrow_made, 1)
                    act.wait_ge(xT_made, c + 1)
                    act.activation(xT[:, b], xT_ps[:, b], ACT.Copy).then_inc(xT_copied, 1)
                    for s in range(TPC):
                        t = c * TPC + s
                        act.wait_ge(v_taken, t + 3)
                        act.wait_ge(dots_made, t + 1)
                        act.activation(prods[:, s % 2, 2], nat_ps[:, s % 2, 2 * D:3 * D], ACT.Square
                                       ).then_inc(kk_made, 1)
                    for h in range(HEADS):
                        act.wait_ge(k_made, c * HEADS + h + 1 + 2 * HEADS)
                        act.activation(G["Kst"][0:3 * C, h, bass.ds(c * CHUNK, CHUNK)], k_ps[0:3 * C, h],
                                       ACT.Identity, bias=bk3[:, h:h + 1]).then_inc(k_high, 1)
            for a in range(2):
                act.wait_ge(shift_turned, a + 1)
                act.activation(shiftT[:, a], xT_ps[:, a, 0:P], ACT.Copy).then_inc(shift_copied, 1)

        @block.vector
        def _(dve):
            chain = Chain(dve, step)
            dve.wait_ge(w_in, 9 * 16)
            for r in range(3):
                last = dve.tensor_copy(Wk3[:, :, r], Wvqk[:, 2 * D:3 * D].rearrange("p (h c) -> p h c", h=HEADS))
            last.then_inc(w_made, 1)
            for start, n in ((v_taken, 2), (dots_made, 2), (k_low, HEADS)):
                dve.sem_inc(start, n)
            with dve.Fori(0, CHUNKS // 2) as cc:
                for half in range(2):
                    c = 2 * cc + half
                    for s in range(TPC):
                        t = c * TPC + s
                        b = s % 2
                        dve.wait_ge(nat_made, t + 1)
                        dve.wait_ge(dots_made, t + 1)
                        dve.tensor_tensor(qrow[:, b], nat_ps[:, b, D:2 * D], rows[:, 1], ALU.add).then_inc(q_made, 1)
                        dve.tensor_tensor(G["v"][:, bass.ds(t, 1)].rearrange("p a f -> p (a f)"),
                                          nat_ps[:, b, 0:D], rows[:, 0], ALU.add).then_inc(v_taken, 1)
                        dve.wait_ge(q_made, t + 1)
                        dve.tensor_tensor(prods[:, b, 0], qrow[:, b], qrow[:, b], ALU.mult)
                        dve.tensor_tensor(prods[:, b, 1], qrow[:, b], rows[:, 2], ALU.mult).then_inc(prods_made, 1)
                        dve.wait_ge(prods_made, t + 1)
                        dve.wait_ge(kk_made, t + 3)
                        dve.tensor_reduce(dots[:, bass.ds(t, 1)].rearrange("p t a h -> p (t a h)"),
                                          prods[:, b].rearrange("p a (h c) -> p (a h) c", h=HEADS), AX.X, ALU.add
                                          ).then_inc(dots_made, 1)
                    for h in range(HEADS):
                        dve.wait_ge(k_high, c * HEADS + h + 1)
                        low = G["Kst"][C:2 * C, h, bass.ds(c * CHUNK, CHUNK)]
                        dve.scalar_tensor_tensor(out=low, in0=k_ps[C:2 * C, h], scalar=bk3[C:2 * C, h:h + 1],
                                                 in1=low, op0=ALU.add, op1=ALU.subtract).then_inc(k_low, 1)
            dve.wait_ge(dots_made, TILES + 2)
            dve.tensor_reduce(kmax[:, 0], dots[:, :, 2].rearrange("p t h -> p h t"), AX.X, ALU.max).then_inc(kpart, 1)
            dve.wait_ge(kall, 1)
            chain(dve.tensor_tensor(guard[:], dots[:, :, 0].rearrange("p t h -> p h t"),
                                    bcast(kmax[:, 1].unsqueeze(2), [P, HEADS, TILES]), ALU.mult))
            rsqrt_newton(chain, dve, root[:], guard[:], tmp[:])
            chain(dve.tensor_tensor(guard[:], guard[:], root[:], ALU.mult))
            chain(dve.tensor_tensor(guard[:], guard[:], dots[:, :, 1].rearrange("p t h -> p h t"), ALU.add))
            dve.tensor_scalar(shift[:].rearrange("p c h s -> p h c s"),
                              guard[:].rearrange("p h (c s) -> p h c s", s=TPC), -1.0, None, ALU.mult
                              ).then_inc(shift_made, 1)




def layer1(nc, io, G):
    NP = 4
    LAG = 3
    LOADS = 2
    HALF = 8
    TURNS = PAIRS // LOADS
    HS = TURNS * HALF
    EPI_STEPS = 15 + RSQRT_STEPS
    with ExitStack() as ctx:
        sb = lambda n, s, d=F32: ctx.enter_context(nc.sbuf_tensor(n, s, d))
        ps = lambda n, s, d=F32: ctx.enter_context(nc.psum_tensor(n, s, d))
        sem = lambda n: ctx.enter_context(nc.semaphore(n))
        adj = sb("adj1", [P, LOADS, 2, CHUNK])
        prob = sb("prob", [P, NP, 2, CHUNK])
        Qst = sb("Qst", [KROWS, 2, HEADS, CHUNK], FP16)
        xrow = sb("xrow1", [P, TPC, D])
        xT = sb("xT1", [P, CHUNK])
        skip = sb("skip", [P, 2, TPC, D])
        stage = sb("stage", [P, 2, HEADS, VW])
        Wq = sb("Wq_", [P, D])
        Wq3 = sb("Wq3", [P, HEADS, 3, C])
        Ws = sb("Ws_", [P, D])
        bq3 = sb("bq3", [3 * C, HEADS])
        bs = sb("bs_", [P, D])
        Wb = sb("Wb_", [P, 3, D])
        outT = sb("outT", [P, 2, CHUNK])
        att = sb("att", [P, TPC, D])
        diff = sb("diff", [P, TPC, D])
        gates = sb("gates", [P, TPC, 3, D])
        den = sb("den", [P, 2, TPC, HEADS])
        z = sb("z", [P, 2, TPC])
        stats = sb("stats1", [P, TPC, 6])
        mv = sb("mv1", [P, TPC, 2])
        rstd = sb("rstd", [P, 3, TPC])
        y = sb("y", [P, TPC, D])
        sc = ps("sc", [P, 2, 2, CHUNK])
        acc = ps("acc1", [P, 2, CHUNK])
        misc = ps("misc", [P, 2, CHUNK])
        adj_in = [sem(f"adj1_in{k}") for k in range(LOADS)]
        apart, pool_apart, y_free = sem("apart1"), sem("pool_apart"), sem("y_free")
        (w_in, w_made, scored, probed, masked, summed, staged, stage_init, acc_done, acc_copied, turned,
         xrow_made, xT_made, xT_copied, q_made, q_high, q_low, skip_summed, skip_made, shift_in, step, att_made,
         z_made, ez_made, y_made, y_out, pool_step) = (sem(n) for n in (
             "w1_in", "w1_made", "scored", "probed", "masked", "summed", "staged", "stage_init", "acc_done",
             "acc_copied", "turned", "xrow1_made", "xT1_made", "xT1_copied", "q1_made", "q_high", "q_low",
             "skip_summed", "skip_made", "shift_in", "step1", "att_made", "z_made", "ez_made", "y_made", "y_out",
             "pool_step1"))
        out_rows = io["out"].rearrange("(p t) f -> p t f", p=P)
        shift_rows = io["shift"].rearrange("(c r) q -> c (r q)", c=CHUNKS)
        block = ctx.enter_context(nc.Block())

        RUNS = [(1, 3), (3, 5), (5, 7), (7, 9), (9, 11), (11, 13), (13, TURNS)]

        def runs(eng, turn_body, pieces):
            for (lo, hi), piece in zip(RUNS, pieces + [()] * (len(RUNS) - len(pieces))):
                with eng.Fori(lo, hi) as j:
                    turn_body(j)
                for part in piece:
                    part()
                if piece and eng is nc.vector:
                    eng.sem_inc(apart, 1)

        @block.sync
        def _(sp):
            for dst, src in ((Wq[:], io["Wq"]), (Ws[:], io["Ws"]), (bs[:], io["bs"].partition_broadcast(P)),
                             (Wb[:].rearrange("p a f -> p (a f)"),
                              io["Wb"].rearrange("a b -> (a b)").partition_broadcast(P))):
                sp.dma_start(dst, src).then_inc(w_in, 16)
            for r in range(3):
                sp.dma_start(bq3[r * C:(r + 1) * C], io["bq_c"]).then_inc(w_in, 16)
            with sp.Fori(0, CHUNKS * TURNS) as turn:
                for k in range(LOADS):
                    sp.wait_ge(masked, turn * HALF + 4 * k + 4)
                    sp.dma_start(adj[:, k].rearrange("p a w -> p (a w)"),
                                 io["adj"][bass.ds(turn * LOADS + k, 1)].rearrange("a p w -> (a p) w")
                                 ).then_inc(adj_in[k], 16)

        @block.gpsimd
        def _(pool):
            pool.memset(stage[:], 0.0).then_inc(pool_step, 1)
            pool.wait_ge(pool_step, 1)
            pool.memset(stage[:, :, :, C:C + 1], 1.0).then_inc(stage_init, 1)
            pool.dma_start(Qst[3 * C:KROWS, 0].rearrange("p h w -> p (h w)"), shift_rows[0:1]).then_inc(shift_in, 16)
            pool.wait_ge(stage_init, 1)
            pool.sem_inc(y_free, 1)

            def stage_values(c, lo, hi):
                with pool.Fori(lo, hi) as j:
                    for b in range(2):
                        wait_apart(pool, summed, (c * TILES + 2 * j + b) * 2 + 2, pool_apart)
                        pool.tensor_copy(stage[:, b, :, 0:C],
                                         G["v"][:, bass.ds(2 * j + b, 1)].rearrange("p a (h c) -> p (a h) c", h=HEADS)
                                         ).then_inc(staged, 1)

            def next_shift(c):
                pool.dma_start(Qst[3 * C:KROWS, bass.ds((c + 1) % 2, 1)].rearrange("p a h w -> p (a h w)"),
                               shift_rows[bass.ds((c + 1) % CHUNKS, 1)]).then_inc(shift_in, 16)

            def store(n):
                pool.wait_ge(y_made, n + 1)
                pool.dma_start(out_rows[:, bass.ds(n * TPC, TPC)], y[:]).then_inc(y_out, 16)

            stage_values(0, 0, 4)
            next_shift(0)
            stage_values(0, 4, TILES // 2)
            with pool.Fori(1, CHUNKS) as c:
                stage_values(c, 0, 4)
                next_shift(c)
                stage_values(c, 4, TILES // 2 - 1)
                store(c - 1)
                stage_values(c, TILES // 2 - 1, TILES // 2)
                pool.wait_ge(y_out, 16 * c)
                pool.sem_inc(y_free, 1)
            store(CHUNKS - 1)
            pool.wait_ge(shift_in, 16 * (CHUNKS + 1))
            pool.wait_ge(y_out, 16 * CHUNKS)

        @block.tensor
        def _(pe):
            def score(c, turn, k):
                pe.wait_ge(probed, c * HS + turn * HALF + k + 1)
                for hh in range(2):
                    h = 2 * (k % 2) + hh
                    last = pe.matmul(sc[:, k % 2, hh], G["Kst"][:, h, bass.ds((turn * (HALF // 2) + k // 2) * P, P)],
                                     Qst[:, bass.ds(c % 2, 1), h].rearrange("p a w -> p (a w)"),
                                     start=True, stop=True)
                last.then_inc(scored, 1)

            def weigh(c, turn, k):
                pe.wait_ge(masked, c * HS + turn * HALF + k + HALF + 1)
                if k % 2 == 0:
                    pe.wait_ge(staged, c * TILES + turn * (HALF // 2) + k // 2 + 1)
                for hh in range(2):
                    last = pe.matmul(acc[hh * VW:(hh + 1) * VW, k % 2], stage[:, (k // 2) % 2, 2 * (k % 2) + hh],
                                     prob[:, k % NP, hh], start=False, stop=False)
                last.then_inc(summed, 1)

            def step_of(c, turn, k):
                score(c, turn, k)
                weigh(c, turn if k >= LAG else turn - 1, (k - LAG) % HALF)

            def edge(c, start):
                for pair in range(2):
                    last = pe.matmul(acc[:, pair], G["zeros"][:, 0:P], G["zeros"][:, 0:CHUNK], start=start,
                                     stop=not start)
                return last

            def turn_source(n):
                pe.wait_ge(xrow_made, n + 1)
                for s in range(TPC):
                    last = pe.transpose(misc[:, 0, s * P:(s + 1) * P], xrow[:, s], G["ident"][:])
                last.then_inc(xT_made, 1)

            def queries(n, heads):
                pe.wait_ge(xT_copied, n + 1)
                for h in heads:
                    if h >= 2:
                        pe.wait_ge(q_low, n * HEADS + h - 1)
                    pe.matmul(misc[0:3 * C, (h + 1) % 2], Wq3[:, h].rearrange("p a c -> p (a c)"), xT[:],
                              start=True, stop=True).then_inc(q_made, 1)

            def skips(n):
                pe.wait_ge(q_low, n * HEADS + HEADS)
                for s in range(TPC):
                    last = pe.matmul(misc[:, 1, s * P:(s + 1) * P], xT[:, s * P:(s + 1) * P], Ws[:],
                                     start=True, stop=True)
                last.then_inc(skip_summed, 1)

            def turn_out(n):
                pe.wait_ge(acc_copied, n + 2)
                for s in range(TPC):
                    for pair in range(2):
                        last = pe.transpose(misc[:, s // 2, (s % 2) * 2 * P + pair * P:(s % 2) * 2 * P + (pair + 1) * P],
                                            outT[:, pair, s * P:(s + 1) * P], G["ident"][:])
                last.then_inc(turned, 1)

            def chunk(c, first):
                pe.wait_ge(q_low, (c + 1) * HEADS)
                pe.wait_ge(shift_in, c * 16 + 16)
                for k in range(LAG):
                    score(c, 0, k)
                pe.wait_ge(acc_copied, c + 1)
                edge(c, True)
                for k in range(LAG, HALF):
                    step_of(c, 0, k)

                def turn_body(j):
                    for k in range(HALF):
                        step_of(c, j, k)

                def after_epilogue():
                    if not first:
                        pe.wait_ge(att_made, c)
                runs(pe, turn_body, [
                    [] if first else [lambda: turn_out(c - 1)],
                    [after_epilogue, lambda: turn_source(c + 1)],
                    [lambda: queries(c + 1, (0, 1))],
                    [lambda: queries(c + 1, (2, 3))],
                    [lambda: skips(c + 1)],
                ])
                for k in range(HALF - LAG, HALF):
                    weigh(c, TURNS - 1, k)
                edge(c, False).then_inc(acc_done, 1)

            pe.sem_inc(summed, 4)
            pe.wait_ge(w_made, 1)
            turn_source(0)
            queries(0, range(HEADS))
            skips(0)
            chunk(0, True)
            with pe.Fori(1, CHUNKS) as c:
                chunk(c, False)
            turn_out(CHUNKS - 1)

        @block.scalar
        def _(act):
            def turn_body(c, j):
                for k in range(HALF):
                    act.wait_ge(scored, c * HS + j * HALF + k + 1)
                    act.activation(prob[:, k % NP].rearrange("p a w -> p (a w)"),
                                   sc[:, k % 2].rearrange("p a w -> p (a w)"), ACT.Exp, scale=SCALE
                                   ).then_inc(probed, 1)

            def copy_source(n):
                act.wait_ge(skip_summed, n + 1)
                act.activation(xrow[:], G["x1"][:, bass.ds((n % CHUNKS) * TPC, TPC)], ACT.Copy).then_inc(xrow_made, 1)

            def copy_turned(n):
                act.wait_ge(xT_made, n + 1)
                act.activation(xT[:], misc[:, 0], ACT.Copy).then_inc(xT_copied, 1)

            def high(n, heads):
                for h in heads:
                    act.wait_ge(q_made, n * HEADS + h + 1)
                    act.activation(Qst[0:3 * C, bass.ds(n % 2, 1), h].rearrange("p a w -> p (a w)"),
                                   misc[0:3 * C, (h + 1) % 2], ACT.Identity, bias=bq3[:, h:h + 1]).then_inc(q_high, 1)

            def gate(n):
                act.wait_ge(z_made, n + 1)
                act.activation(z[:, 1], z[:, 0], ACT.Exp, scale=-1.0).then_inc(ez_made, 1)

            def chunk(c, first):
                turn_body(c, 0)
                runs(act, lambda j: turn_body(c, j), [
                    [lambda: copy_source(c + 1)],
                    [lambda: copy_turned(c + 1)],
                    [lambda: high(c + 1, (0, 1))],
                    [lambda: high(c + 1, (2, 3))],
                    [] if first else [lambda: gate(c - 1)],
                ])
                act.wait_ge(acc_done, c + 1)
                if not first:
                    act.wait_ge(turned, c)
                act.activation(outT[:], acc[:], ACT.Copy).then_inc(acc_copied, 1)

            act.sem_inc(probed, 2)
            act.sem_inc(acc_copied, 1)
            act.wait_ge(w_in, 7 * 16)
            copy_source(0)
            copy_turned(0)
            high(0, range(HEADS))
            chunk(0, True)
            with act.Fori(1, CHUNKS) as c:
                chunk(c, False)
            gate(CHUNKS - 1)

        @block.vector
        def _(dve):
            def turn_body(c, j):
                for k in range(HALF):
                    dve.wait_ge(probed, c * HS + j * HALF + k + 3)
                    if k % 4 == 0:
                        dve.wait_ge(adj_in[k // 4], (c * TURNS + j) * 16 + 16)
                    m = (k // 2) % 2
                    dve.tensor_tensor(prob[:, k % NP], prob[:, k % NP],
                                      bcast(adj[:, k // 4, m:m + 1], [P, 2, CHUNK]), ALU.mult).then_inc(masked, 1)

            def low(n, heads):
                for h in heads:
                    dve.wait_ge(q_high, n * HEADS + h + 1)
                    rest = Qst[2 * C:3 * C, bass.ds(n % 2, 1), h].rearrange("p a w -> p (a w)")
                    dve.scalar_tensor_tensor(out=rest, in0=misc[2 * C:3 * C, (h + 1) % 2],
                                             scalar=bq3[2 * C:3 * C, h:h + 1], in1=rest, op0=ALU.add,
                                             op1=ALU.subtract).then_inc(q_low, 1)

            def skips(n):
                dve.wait_ge(skip_summed, n + 2)
                dve.tensor_tensor(skip[:, bass.ds(n % 2, 1)].rearrange("p a s f -> p (a s) f"),
                                  misc[:, 1].rearrange("p (s f) -> p s f", s=TPC),
                                  bcast(bs[:].unsqueeze(1), [P, TPC, D]), ALU.add).then_inc(skip_made, 1)

            def attention(chain, n):
                dve.wait_ge(turned, n + 1)
                sums = misc[:].rearrange("p b (s h w) -> p (b s h) w", h=HEADS, w=VW)
                chain(dve.tensor_copy(den[:, 0].rearrange("p s h -> p (s h)").unsqueeze(2), sums[:, :, C:C + 1]))
                chain(dve.tensor_scalar(den[:, 1], den[:, 0], 0.0, None, ALU.is_equal))
                chain(dve.tensor_tensor(den[:, 0], den[:, 0], den[:, 1], ALU.add))
                chain(dve.reciprocal(den[:, 1], den[:, 0]))
                dve.tensor_tensor(att[:].rearrange("p s (c h) -> p s h c", h=HEADS),
                                  misc[:].rearrange("p b (s h w) -> p (b s) h w", h=HEADS, w=VW)[:, :, :, 0:C],
                                  bcast(den[:, 1].unsqueeze(3), [P, TPC, HEADS, C]),
                                  ALU.mult).then_inc(att_made, 1)
                dve.wait_ge(att_made, n + 1)

            def gate_terms(chain, n, which):
                if which == 0:
                    dve.wait_ge(skip_made, n + 1)
                    chain(dve.tensor_tensor(diff[:], att[:], skip[:, bass.ds(n % 2, 1)].rearrange("p a s f -> p (a s) f"),
                                            ALU.subtract))
                part = (att[:], skip[:, bass.ds(n % 2, 1)].rearrange("p a s f -> p (a s) f"), diff[:])[which]
                chain(dve.tensor_tensor(gates[:, :, which], part, bcast(Wb[:, which:which + 1], [P, TPC, D]), ALU.mult))

            def gate_sum(chain, n):
                dve.tensor_reduce(z[:, 0], gates[:].rearrange("p s a f -> p s (a f)"), AX.X, ALU.add).then_inc(z_made, 1)

            def mix(chain, n):
                chain(dve.tensor_tensor(att[:], att[:], G["x1"][:, bass.ds(n * TPC, TPC)], ALU.add))
                dve.wait_ge(ez_made, n + 1)
                chain(dve.tensor_scalar(z[:, 1], z[:, 1], -1.0, -1.0, ALU.mult, ALU.add))
                chain(dve.reciprocal(z[:, 0], z[:, 1]))
                for s in range(TPC):
                    last = dve.scalar_tensor_tensor(out=att[:, s], in0=diff[:, s], scalar=z[:, 0, s:s + 1],
                                                    in1=att[:, s], op0=ALU.mult, op1=ALU.add)
                chain(last)

            def statistics(chain, n):
                for s in range(TPC):
                    last = dve.bn_stats(stats[:, s], att[:, s])
                chain(last)
                dve.sem_inc(apart, 1)
                for s in range(TPC):
                    last = dve.bn_aggr(mv[:, s], stats[:, s])
                chain(last)
                chain(dve.tensor_scalar(rstd[:, 0], mv[:, :, 1], EPS, None, ALU.add))
                rsqrt_newton(chain, dve, rstd[:, 1], rstd[:, 0], rstd[:, 2])

            def norm(chain, n):
                dve.wait_ge(y_free, n + 1)
                for s in range(TPC):
                    last = dve.tensor_scalar(y[:, s], att[:, s], mv[:, s, 0:1], rstd[:, 1, s:s + 1],
                                             ALU.subtract, ALU.mult)
                last.then_inc(y_made, 1)

            def chunk(c, first):
                turn_body(c, 0)
                n = c - 1
                chain = Chain(dve, step, None if first else n * EPI_STEPS)
                runs(dve, lambda j: turn_body(c, j), [
                    [] if first else [lambda: attention(chain, n)],
                    [] if first else [lambda: gate_terms(chain, n, 0)],
                    ([] if first else [lambda: gate_terms(chain, n, 1)]) + [lambda: low(c + 1, (0, 1))],
                    ([] if first else [lambda: gate_terms(chain, n, 2), lambda: gate_sum(chain, n)])
                    + [lambda: low(c + 1, (2, 3))],
                    [lambda: skips_after(c + 1)] + ([] if first else [lambda: mix(chain, n)]),
                    [] if first else [lambda: statistics(chain, n)],
                    [] if first else [lambda: norm(chain, n)],
                ])
                assert first or chain.steps == EPI_STEPS, chain.steps

            def skips_after(n):
                skips(n)

            dve.sem_inc(masked, HALF)
            dve.wait_ge(w_in, 7 * 16)
            for r in range(3):
                last = dve.tensor_copy(Wq3[:, :, r], Wq[:].rearrange("p (h c) -> p h c", h=HEADS))
            last.then_inc(w_made, 1)
            dve.sem_inc(skip_summed, 1)
            low(0, range(HEADS))
            skips(0)
            chunk(0, True)
            with dve.Fori(1, CHUNKS) as c:
                chunk(c, False)
            n = CHUNKS - 1
            chain = Chain(dve, step, n * EPI_STEPS)
            attention(chain, n)
            for which in range(3):
                gate_terms(chain, n, which)
            gate_sum(chain, n)
            mix(chain, n)
            statistics(chain, n)
            norm(chain, n)


def program(nc, io):
    with ExitStack() as ctx:
        sb = lambda n, s, d=F32: ctx.enter_context(nc.sbuf_tensor(n, s, d))
        G = {"ident": sb("ident", [P, P]), "ones": sb("ones", [P, P]), "zeros": sb("zeros", [P, CHUNK], BF16),
             "x1": sb("x1", [P, TILES, D])}
        with ExitStack() as first:
            sb0 = lambda n, s, d=F32: first.enter_context(nc.sbuf_tensor(n, s, d))
            for n in ("f1", "neg_f2", "A", "Cf", "e1", "e2"):
                G[n] = sb0(n, [P, TILES])
            G["F1"] = sb0("F1", [P, N])
            G["XI"] = sb0("XI", [P, TILES, 3, ONE], BF16)
            G["XJ"] = sb0("XJ", [P, TILES, 2, ONE], FP16)
            G["SX"] = sb0("SX", [P, ONE])
            node_logits(nc, io, G)
            source_factors(nc, io, G)
            layer0(nc, io, G)
        G["Kst"] = sb("Kst", [KROWS, HEADS, N], FP16)
        G["v"] = sb("v", [P, TILES, D])
        projections(nc, io, G)
        layer1(nc, io, G)


_NAMES = {"x": "x", "inl": "L0_gnn_inlayer2", "W1": "L0_gnn_W1", "w2": "L0_gnn_w2", "w3": "L0_gnn_w3",
          "b2": "L0_gnn_b2", "b3": "L0_gnn_b3", "Wq": "L1_gnn_Wq", "bq": "L1_gnn_bq", "Wk": "L1_gnn_Wk",
          "bk": "L1_gnn_bk", "Wv": "L1_gnn_Wv", "bv": "L1_gnn_bv", "Ws": "L1_gnn_Ws", "bs": "L1_gnn_bs",
          "Wb": "L1_gnn_Wb"}


def kernel(**inputs):
    import numpy as np
    import concourse.bacc as bacc
    from concourse.bass_utils import run_bass_kernel_spmd

    arrays = {k: np.asarray(inputs[name]) for k, name in _NAMES.items()}
    for k in ("b2", "b3"):
        arrays[k] = arrays[k].reshape(1, 1)
    for k in ("bq", "bk"):
        arrays[k + "_c"] = arrays[k].reshape(HEADS, C).T
    adj = np.asarray(inputs["adj"]).reshape(P, CHUNKS, TPC, P, PAIRS, 2)
    arrays["adj"] = adj.transpose(1, 4, 3, 5, 2, 0).reshape(CHUNKS * PAIRS, P, PAIR_W)
    nc = bacc.Bacc("TRN2", target_bir_lowering=False, num_devices=1)
    io, sent = {}, {}
    for k, a in arrays.items():
        sent[f"in_{k}_dram"] = np.ascontiguousarray(a)
        io[k] = nc.dram_tensor(f"in_{k}_dram", a.shape, mybir.dt.from_np(a.dtype), kind="ExternalInput").ap()
    io["out"] = nc.dram_tensor("out_dram", (N, D), F32, kind="ExternalOutput").ap()
    io["shift"] = nc.dram_tensor("shift_dram", (CHUNKS * HEADS * TPC, P), FP16, kind="Internal").ap()
    program(nc, io)
    return run_bass_kernel_spmd(nc, [sent], core_ids=[0]).results[0]["out_dram"]
```

```python
from contextlib import ExitStack

import concourse.bass as bass
import concourse.mybir as mybir
from concourse.alu_op_type import AluOpType as ALU

F32 = mybir.dt.float32
BF16 = mybir.dt.bfloat16
FP16 = mybir.dt.float16
I32 = mybir.dt.int32
ACT = mybir.ActivationFunctionType
AX = mybir.AxisListType

P = 128
N = 8192
D = 128
HEADS = 4
C = D // HEADS
TILES = N // P
TPC = 4
CHUNK = TPC * P
CHUNKS = N // CHUNK
PAIRS = TILES // 2
PAIR_W = 2 * CHUNK
ONE = D + 1
SLOPE = 0.01
EPS = 1e-5
SCALE = float(C) ** -0.5
RSQRT_MAGIC = 1597463007.0
VW = 64
KROWS = 3 * C + 1


class Chain:

    def __init__(self, eng, sem, start=0):
        self.eng, self.sem, self.n = eng, sem, start
        self.steps = 0

    def __call__(self, ins):
        ins.then_inc(self.sem, 1)
        self.n = self.n + 1
        self.steps += 1
        self.eng.wait_ge(self.sem, self.n)


def wait_apart(eng, sem, value, mark):
    eng.wait_ge(sem, value)
    eng.sem_inc(mark, 1)


def bcast(ap, shape):
    return ap.to_broadcast(shape)


def rsqrt_newton(chain, dve, out, v, tmp):
    chain(dve.tensor_scalar(out.bitcast(I32), v.bitcast(I32), -0.5, RSQRT_MAGIC, ALU.mult, ALU.add))
    for _ in range(3):
        chain(dve.tensor_tensor(tmp, out, out, ALU.mult))
        chain(dve.scalar_tensor_tensor(out=tmp, in0=tmp, scalar=-0.5, in1=v, op0=ALU.mult, op1=ALU.mult))
        chain(dve.scalar_tensor_tensor(out=out, in0=tmp, scalar=1.5, in1=out, op0=ALU.add, op1=ALU.mult))


RSQRT_STEPS = 10


def node_logits(nc, io, G):
    GT = 8
    NG = TILES // GT
    with ExitStack() as ctx:
        sb = lambda n, s, d=F32: ctx.enter_context(nc.sbuf_tensor(n, s, d))
        ps = lambda n, s, d=F32: ctx.enter_context(nc.psum_tensor(n, s, d))
        sem = lambda n: ctx.enter_context(nc.semaphore(n))
        inl = sb("inl", [P, 2, GT, 2 * D])
        junk = sb("junk", [P, 4, 2 * D])
        W1 = sb("W1", [P, 2 * D])
        wcol = sb("wcol", [P, 2])
        bcol = sb("bcol", [P, 2])
        wrow = sb("wrow", [P, 2, P])
        ub = sb("ub", [P, 2, 2 * D])
        f = sb("f", [P, 2, TILES])
        s = sb("s", [P, TILES])
        s_small = sb("s_small", [P, TILES])
        s_max = sb("s_max", [P, TILES])
        gmax = sb("gmax", [P, 4])
        diag = sb("diag", [P, 2, CHUNK])
        u_ps = ps("u_ps", [P, 2, 2 * D])
        f_ps = ps("f_ps", [P, 2, CHUNK])
        weights_in, inl_in0, inl_in1 = sem("weights_in"), sem("inl_in0"), sem("inl_in1")
        inl_in = [inl_in0, inl_in1]
        dots_done, consts_ready, wrow_ready, u_done, ub_ready = (
            sem("dots_done"), sem("consts_ready"), sem("wrow_ready"), sem("u_done"), sem("ub_ready"))
        dve_step, act_step, pool_step = sem("dve_step"), sem("act_step"), sem("pool_step")
        f_ready, gpart_ready, gmax_ready, args_ready = (
            sem("f_ready"), sem("gpart_ready"), sem("gmax_ready"), sem("args_ready"))
        diag_ready, f_bcast, f_copied = sem("diag_ready"), sem("f_bcast"), sem("f_copied")
        x_in = sem("x_in")
        block = ctx.enter_context(nc.Block())

        @block.sync
        def _(sp):
            sp.dma_start(W1[:], io["W1"]).then_inc(weights_in, 16)
            for i, k in enumerate(("w2", "w3")):
                sp.dma_start(wcol[:, i:i + 1], io[k].rearrange("(p a) -> p a", a=1)).then_inc(weights_in, 16)
            for i, k in enumerate(("b2", "b3")):
                sp.dma_start(bcol[:, i:i + 1], io[k].partition_broadcast(P).rearrange("p a b -> p (a b)")
                             ).then_inc(weights_in, 16)
            src = io["inl"].rearrange("(p g t) f -> g p (t f)", p=P, g=NG)
            with sp.Fori(0, NG // 2) as gg:
                for b in range(2):
                    sp.wait_ge(dots_done, (2 * gg + b) * (2 * GT) + 2 * GT)
                    sp.dma_start(inl[:, b].rearrange("p t f -> p (t f)"),
                                 src[bass.ds(2 * gg + b, 1)].rearrange("a p w -> (a p) w")).then_inc(inl_in[b], 16)

        @block.gpsimd
        def _(pool):
            chain = Chain(pool, pool_step)
            chain(pool.memset(G["ident"][:], 0.0))
            pool.affine_select(out=G["ident"][:], in_=G["ident"][:], compare_op=ALU.not_equal, fill=1.0,
                               base=0, pattern=[[-1, P]], channel_multiplier=1).then_inc(consts_ready, 1)
            pool.memset(G["ones"][:], 1.0).then_inc(consts_ready, 1)
            src = io["x"].rearrange("(p t) f -> p t f", p=P)
            for g in range(4):
                tiles = slice(g * TILES // 4, (g + 1) * TILES // 4)
                pool.wait_ge(dots_done, 4 * GT + 1 + g * 4 * GT)
                pool.dma_start(G["x1"][:, tiles], src[:, tiles]).then_inc(x_in, 16)
            pool.wait_ge(gpart_ready, 1)
            pool.partition_all_reduce(gmax[:, 1:2], gmax[:, 0:1], P, bass.bass_isa.ReduceOp.max
                                      ).then_inc(gmax_ready, 1)
            pool.wait_ge(x_in, 4 * 16)

        @block.vector
        def _(dve):
            chain = Chain(dve, dve_step)
            dve.sem_inc(dots_done, 4 * GT)
            dve.wait_ge(weights_in, 5 * 16)
            dve.wait_ge(consts_ready, 2)
            for i in range(2):
                dve.tensor_scalar(wrow[:, i], G["ones"][:], wcol[:, i:i + 1], None, ALU.mult
                                  ).then_inc(wrow_ready, 1)
            dve.wait_ge(ub_ready, 1)
            with dve.Fori(0, NG // 2) as gg:
                for b in range(2):
                    dve.wait_ge(inl_in[b], gg * 16 + 16)
                    for k in range(2 * GT):
                        t, i = k // 2, k % 2
                        dve.wait_ge(dots_done, (2 * gg + b) * (2 * GT) + k + 4 * GT - 3)
                        dve.scalar_tensor_tensor(
                            out=junk[:, k % 4], in0=inl[:, b, t], scalar=1.0, in1=ub[:, i], op0=ALU.mult,
                            op1=ALU.mult, accum_out=f[:, i, bass.ds((2 * gg + b) * GT + t, 1)]
                        ).then_inc(dots_done, 1)
            dve.wait_ge(dots_done, 2 * TILES + 4 * GT)
            dve.tensor_scalar(G["f1"][:], f[:, 0], bcol[:, 0:1], None, ALU.add).then_inc(f_ready, 1)
            chain(dve.tensor_scalar(f[:, 1], f[:, 1], bcol[:, 1:2], None, ALU.add))
            dve.reduce_max(gmax[:, 0:1], f[:, 1], AX.X).then_inc(gpart_ready, 1)
            dve.tensor_scalar(G["neg_f2"][:], f[:, 1], -1.0, None, ALU.mult)
            dve.wait_ge(gmax_ready, 1)
            dve.wait_ge(f_ready, 1)
            chain(dve.tensor_scalar(s[:], G["f1"][:], gmax[:, 1:2], None, ALU.add))
            chain(dve.tensor_scalar(s_small[:], s[:], SLOPE, None, ALU.mult))
            chain(dve.tensor_tensor(s_max[:], s[:], s_small[:], ALU.max))
            chain(dve.tensor_tensor(s[:], s[:], s_max[:], ALU.subtract))
            chain(dve.tensor_tensor(s_small[:], s_small[:], s_max[:], ALU.subtract))
            chain(dve.tensor_scalar(gmax[:, 2:3], gmax[:, 1:2], -1.0, None, ALU.mult))
            dve.tensor_scalar(gmax[:, 3:4], gmax[:, 1:2], -SLOPE, None, ALU.mult).then_inc(args_ready, 1)

        @block.scalar
        def _(act):
            act.wait_ge(u_done, 1)
            act.activation(ub[:], u_ps[:], ACT.Copy).then_inc(ub_ready, 1)
            act.sem_inc(f_copied, 2)
            with act.Fori(0, CHUNKS // 2) as cc:
                for b in range(2):
                    c = 2 * cc + b
                    act.wait_ge(f_bcast, c + 1)
                    act.wait_ge(dots_done, c * (2 * TPC) + 2 * TPC + 4 * GT)
                    for k in range(TPC):
                        last = act.activation(diag[:, b, k * P:(k + 1) * P], G["ident"][:], ACT.Copy,
                                              scale=f[:, 0, bass.ds(c * TPC + k, 1)])
                    last.then_inc(diag_ready, 1)
                for b in range(2):
                    c = 2 * cc + b
                    act.wait_ge(f_bcast, c + 3)
                    act.activation(G["F1"][:, bass.ds(c * CHUNK, CHUNK)], f_ps[:, b], ACT.Identity,
                                   bias=bcol[:, 0:1]).then_inc(f_copied, 1)
            act.wait_ge(args_ready, 1)
            for out, arg, scale, bias in ((G["A"], s, 1.0, 0.0), (G["Cf"], s_small, 1.0, 0.0),
                                          (G["e1"], f, 1.0, gmax[:, 2:3]), (G["e2"], f, SLOPE, gmax[:, 3:4])):
                act.activation(out[:], arg[:, 1] if arg is f else arg[:], ACT.Exp, scale=scale, bias=bias)

        @block.tensor
        def _(pe):
            pe.wait_ge(wrow_ready, 2)
            for i in range(2):
                last = pe.matmul(u_ps[:, i], wrow[:, i], W1[:], start=True, stop=True)
            last.then_inc(u_done, 1)
            pe.sem_inc(f_bcast, 2)
            with pe.Fori(0, CHUNKS // 2) as cc:
                for b in range(2):
                    c = 2 * cc + b
                    pe.wait_ge(diag_ready, c + 1)
                    pe.wait_ge(f_copied, c + 1)
                    pe.matmul(f_ps[:, b], G["ones"][:], diag[:, b], start=True, stop=True).then_inc(f_bcast, 1)


def source_factors(nc, io, G):
    GT = 16
    NG = TILES // GT
    with ExitStack() as ctx:
        sb = lambda n, s, d=F32: ctx.enter_context(nc.sbuf_tensor(n, s, d))
        sem = lambda n: ctx.enter_context(nc.semaphore(n))
        full1 = sb("full1", [P, GT, ONE])
        full2 = sb("full2", [P, GT, ONE])
        sum_ps = ctx.enter_context(nc.psum_tensor("sum_ps", [P, D], F32))
        x_summed, full_ready, part_ready, rest_ready, mid_ready, dve_step = (
            sem("x_summed"), sem("full_ready"), sem("part_ready"), sem("rest_ready"),
            sem("mid_ready"), sem("dve_step2"))
        block = ctx.enter_context(nc.Block())

        @block.tensor
        def _(pe):
            for t in range(TILES):
                last = pe.matmul(sum_ps[:], G["ones"][:], G["x1"][:, t], start=(t == 0), stop=(t == TILES - 1))
            last.then_inc(x_summed, 1)

        @block.vector
        def _(dve):
            for g in range(NG):
                if g >= 1:
                    dve.wait_ge(part_ready, 2 * g)
                    dve.wait_ge(mid_ready, g)
                tiles = slice(g * GT, (g + 1) * GT)
                for full, e in ((full1, G["e1"]), (full2, G["e2"])):
                    dve.tensor_tensor(full[:, :, 0:D], G["x1"][:, tiles],
                                      bcast(e[:, tiles].unsqueeze(2), [P, GT, D]), ALU.mult
                                      ).then_inc(dve_step, 1)
                    dve.tensor_copy(full[:, :, D:ONE], e[:, tiles].unsqueeze(2)).then_inc(full_ready, 1)
                dve.wait_ge(part_ready, 2 * g + 1)
                dve.tensor_tensor(full1[:], full1[:], G["XI"][:, tiles, 0], ALU.subtract).then_inc(rest_ready, 1)
                dve.wait_ge(part_ready, 2 * g + 2)
                dve.tensor_tensor(G["XJ"][:, tiles, 1], full2[:], G["XJ"][:, tiles, 0], ALU.subtract
                                  ).then_inc(dve_step, 1)
                dve.wait_ge(mid_ready, g + 1)
                dve.tensor_tensor(G["XI"][:, tiles, 2], full1[:], G["XI"][:, tiles, 1], ALU.subtract
                                  ).then_inc(dve_step, 1)
                dve.wait_ge(dve_step, 4 * (g + 1))
            dve.wait_ge(x_summed, 1)
            dve.tensor_copy(G["SX"][:, 0:D], sum_ps[:])
            dve.memset(G["SX"][:, D:ONE], float(N))

        @block.scalar
        def _(act):
            for g in range(NG):
                tiles = slice(g * GT, (g + 1) * GT)
                act.wait_ge(full_ready, 2 * g + 1)
                act.activation(G["XI"][:, tiles, 0], full1[:], ACT.Copy).then_inc(part_ready, 1)
                act.wait_ge(full_ready, 2 * g + 2)
                act.activation(G["XJ"][:, tiles, 0], full2[:], ACT.Copy).then_inc(part_ready, 1)
                act.wait_ge(rest_ready, g + 1)
                act.activation(G["XI"][:, tiles, 1], full1[:], ACT.Copy).then_inc(mid_ready, 1)


def layer0(nc, io, G):
    NB = 4
    TURNS = PAIRS // NB
    with ExitStack() as ctx:
        sb = lambda n, s, d=F32: ctx.enter_context(nc.sbuf_tensor(n, s, d))
        sem = lambda n: ctx.enter_context(nc.semaphore(n))
        adj = sb("adj", [P, NB, PAIR_W])
        mask = sb("mask", [P, NB, PAIR_W], BF16)
        pos = sb("pos", [P, NB, PAIR_W], BF16)
        neg = sb("neg", [P, NB, PAIR_W], BF16)
        sums = sb("sums", [P, TPC, 5, ONE])
        small = sb("small", [P, 2, TPC])
        stats = sb("stats", [P, TPC, 6])
        mv = sb("mv", [P, TPC, 2])
        mvs = sb("mvs", [P, TILES, 2])
        var = sb("var", [P, 2, TILES])
        acc = ctx.enter_context(nc.psum_tensor("acc0", [P, TPC, 1024], F32))
        adj_in = [sem(f"adj_in{k}") for k in range(NB)]
        mask_made, pos_done, neg_made, masks_free = (
            sem("mask_made"), sem("pos_done"), sem("neg_made"), sem("masks_free"))
        apart = sem("apart0")
        summed, banks_free, sums_free, added, dve_step = (sem(n) for n in (
            "summed0", "banks_free", "sums_free", "added", "dve_step3"))
        pool_apart = sem("pool_apart2")
        ADDS = 4
        block = ctx.enter_context(nc.Block())

        RUNS = [(0, 4), (4, 5), (5, 6), (6, 7), (7, TURNS)]

        @block.sync
        def _(sp):
            with sp.Fori(0, CHUNKS * TURNS) as turn:
                for k in range(NB):
                    sp.wait_ge(mask_made, turn * NB + k + 1)
                    sp.dma_start(adj[:, k], io["adj"][bass.ds(turn * NB + k, 1)].rearrange("a p w -> (a p) w")
                                 ).then_inc(adj_in[k], 16)

        @block.gpsimd
        def _(pool):
            with pool.Fori(0, CHUNKS) as n:
                wait_apart(pool, banks_free, (n + 2) * TPC, pool_apart)
                for i, (to, part) in enumerate(((2, 1), (4, 3), (2, 0), (2, 4))):
                    pool.tensor_tensor(sums[:, :, to], sums[:, :, to], sums[:, :, part], ALU.add).then_inc(added, 1)
                    wait_apart(pool, added, n * ADDS + i + 1, pool_apart)

        @block.scalar
        def _(act):
            def turn_body(turn):
                for k in range(NB):
                    act.wait_ge(adj_in[k], turn * 16 + 16)
                    act.wait_ge(neg_made, turn * NB + k + 1)
                    act.activation(mask[:, k], adj[:, k], ACT.Copy).then_inc(mask_made, 1)

            def evacuate(n):
                act.wait_ge(sums_free, n + 1)
                for s in range(TPC):
                    act.wait_ge(summed, n * TPC + s + 1)
                    part = act.activation(sums[:, s, 0:3].rearrange("p a f -> p (a f)"), acc[:, s, 0:3 * ONE],
                                          ACT.Copy, scale=G["A"][:, bass.ds(n * TPC + s, 1)])
                    if s == TPC - 1:
                        part.then_inc(masks_free, 1)
                    act.activation(sums[:, s, 3:5].rearrange("p a f -> p (a f)"),
                                   acc[:, s, 512:512 + 2 * ONE], ACT.Copy,
                                   scale=G["Cf"][:, bass.ds(n * TPC + s, 1)]).then_inc(banks_free, 1)

            act.sem_inc(mask_made, NB)
            act.sem_inc(banks_free, TPC)
            with act.Fori(0, TURNS) as turn:
                turn_body(turn)
            with act.Fori(1, CHUNKS) as c:
                turn_body(c * TURNS)
                evacuate(c - 1)
                with act.Fori(1, TURNS) as j:
                    turn_body(c * TURNS + j)
            evacuate(CHUNKS - 1)

        @block.vector
        def _(dve):
            def make_pos(c, j, k):
                dve.wait_ge(mask_made, (c * TURNS + j) * NB + k + 1 + NB)
                dve.wait_ge(masks_free, (c * TURNS + j) * NB + k + 1)
                for m in range(2):
                    w = slice(m * CHUNK, (m + 1) * CHUNK)
                    last = dve.scalar_tensor_tensor(
                        out=pos[:, k, w], in0=G["F1"][:, bass.ds(c * CHUNK, CHUNK)],
                        scalar=G["neg_f2"][:, bass.ds(j * (2 * NB) + 2 * k + m, 1)], in1=mask[:, k, w],
                        op0=ALU.is_gt, op1=ALU.mult)
                last.then_inc(pos_done, 1)

            def make_neg(c, j, k):
                dve.wait_ge(pos_done, (c * TURNS + j) * NB + k + 1)
                dve.tensor_tensor(neg[:, k], mask[:, k], pos[:, k], ALU.subtract).then_inc(neg_made, 1)

            def turn_body(c, j):
                make_pos(c, j, 0)
                for k in range(1, NB):
                    make_pos(c, j, k)
                    make_neg(c, j, k - 1)
                make_neg(c, j, NB - 1)

            def fill_empty(chain, n):
                dve.wait_ge(added, (n + 1) * ADDS)
                chain(dve.tensor_scalar(small[:, 0], sums[:, :, 2, D], 0.0, None, ALU.is_equal))
                for s in range(TPC):
                    last = dve.scalar_tensor_tensor(out=sums[:, s, 2], in0=G["SX"][:], scalar=small[:, 0, s:s + 1],
                                                    in1=sums[:, s, 2], op0=ALU.mult, op1=ALU.add)
                chain(last)
                chain(dve.reciprocal(small[:, 1], sums[:, :, 2, D]))

            def residual(chain, n):
                for s in range(TPC):
                    row = G["x1"][:, bass.ds(n * TPC + s, 1)].rearrange("p a f -> p (a f)")
                    last = dve.scalar_tensor_tensor(out=row, in0=sums[:, s, 2, 0:D], scalar=small[:, 1, s:s + 1],
                                                    in1=row, op0=ALU.mult, op1=ALU.add)
                chain(last)
                dve.sem_inc(sums_free, 1)

            def statistics(chain, n):
                for s in range(TPC):
                    last = dve.bn_stats(stats[:, s], G["x1"][:, bass.ds(n * TPC + s, 1)].rearrange("p a f -> p (a f)"))
                chain(last)

            def mean_variance(chain, n):
                for s in range(TPC):
                    last = dve.bn_aggr(mv[:, s], stats[:, s])
                chain(last)
                chain(dve.tensor_copy(mvs[:, bass.ds(n * TPC, TPC)], mv[:]))

            PIECES = [fill_empty, residual, statistics, mean_variance]
            STEPS = 7

            dve.sem_inc(neg_made, NB)
            dve.sem_inc(sums_free, 1)
            with dve.Fori(0, TURNS) as j:
                turn_body(0, j)
            with dve.Fori(1, CHUNKS) as c:
                chain = Chain(dve, dve_step, (c - 1) * STEPS)
                for i, (lo, hi) in enumerate(RUNS):
                    with dve.Fori(lo, hi) as j:
                        turn_body(c, j)
                    if i < len(PIECES):
                        PIECES[i](chain, c - 1)
                        dve.sem_inc(apart, 1)
                assert chain.steps == STEPS
            n = CHUNKS - 1
            chain = Chain(dve, dve_step, n * STEPS)
            for piece in PIECES:
                piece(chain, n)
                dve.sem_inc(apart, 1)
            chain(dve.tensor_scalar(var[:, 0], mvs[:, :, 1], EPS, None, ALU.add))
            rsqrt_newton(chain, dve, G["rstd"][:], var[:, 0], var[:, 1])
            dve.scalar_tensor_tensor(out=G["nmr"][:], in0=mvs[:, :, 0], scalar=-1.0, in1=G["rstd"][:],
                                     op0=ALU.mult, op1=ALU.mult)

        @block.tensor
        def _(pe):
            def multiply(k, m, s, t, start, stop):
                w = slice(m * CHUNK + s * P, m * CHUNK + (s + 1) * P)
                xi = G["XI"][:, bass.ds(t, 1)].rearrange("p a k f -> p (a k f)")
                xj = G["XJ"][:, bass.ds(t, 1)].rearrange("p a k f -> p (a k f)")
                pe.matmul(acc[:, s, 0:3 * ONE], pos[:, k, w], xi, start=start, stop=stop)
                return pe.matmul(acc[:, s, 512:512 + 2 * ONE], neg[:, k, w], xj, start=start, stop=stop)

            def load(c, j, k):
                pe.wait_ge(neg_made, (c * TURNS + j) * NB + k + 1 + NB)
                for m in range(2):
                    for s in range(TPC):
                        last = multiply(k, m, s, j * (2 * NB) + 2 * k + m, False, False)
                last.then_inc(masks_free, 1)

            pe.sem_inc(masks_free, NB)
            with pe.Fori(0, CHUNKS) as c:
                pe.wait_ge(neg_made, c * TURNS * NB + 1 + NB)
                for s in range(TPC):
                    pe.wait_ge(banks_free, c * TPC + s + 1)
                    for m in range(2):
                        last = multiply(0, m, s, m, m == 0, False)
                last.then_inc(masks_free, 1)
                for k in range(1, NB):
                    load(c, 0, k)
                with pe.Fori(1, TURNS - 1) as j:
                    for k in range(NB):
                        load(c, j, k)
                for k in range(NB - 1):
                    load(c, TURNS - 1, k)
                pe.wait_ge(neg_made, (c * TURNS + TURNS) * NB + NB)
                for s in range(TPC):
                    for m in range(2):
                        last = multiply(NB - 1, m, s, TILES - 2 + m, False, m == 1)
                    last.then_inc(summed, 1)


def projections(nc, io, G):
    with ExitStack() as ctx:
        sb = lambda n, s, d=F32: ctx.enter_context(nc.sbuf_tensor(n, s, d))
        ps = lambda n, s, d=F32: ctx.enter_context(nc.psum_tensor(n, s, d))
        sem = lambda n: ctx.enter_context(nc.semaphore(n))
        xT = sb("xT", [P, 2, CHUNK])
        Wvqk = sb("Wvqk", [P, 3 * D])
        xrow = sb("xrow", [P, 2, TPC, D])
        Wk3 = sb("Wk3", [P, HEADS, KROWS])
        bk3 = sb("bk3", [KROWS, HEADS])
        rows = sb("rows", [P, 3, D])
        prods = sb("prods", [P, 2, TPC, 3, D])
        qrow = sb("qrow", [P, 2, TPC, D])
        dots = sb("dots", [P, TILES, 3, HEADS])
        guard = sb("guard", [P, HEADS, TILES])
        tmp = sb("tmp", [P, HEADS, TILES])
        root = sb("root", [P, HEADS, TILES])
        kmax = sb("kmax", [P, 2, HEADS])
        shift = sb("shift", [P, CHUNKS, HEADS, TPC])
        shiftT = sb("shiftT", [P, 2, P], FP16)
        xT_ps = ps("xT_ps", [P, 2, CHUNK])
        nat_ps = ps("nat_ps", [P, TPC, 512])
        k_ps = ps("k_ps", [P, 2, CHUNK])
        (w_in, w_made, xT_made, xT_copied, nat_made, v_taken, q_made, prods_made, kk_made, dots_made, k_made,
         k_high, k_low, xrow_made, step, kpart, kall, shift_made, shift_turned, shift_copied, shift_out, x1_stored, pool_apart, pool_step) = (sem(n) for n in (
             "w_in", "w_made", "xT_made", "xT_copied", "nat_made", "v_taken", "q_made", "prods_made",
             "kk_made", "dots_made", "k_made", "k_high", "k_low", "xrow_made", "pstep", "kpart", "kall", "shift_made",
             "shift_turned", "shift_copied", "shift_out", "x1_stored", "pool_apart0", "pool_step0"))
        block = ctx.enter_context(nc.Block())

        @block.sync
        def _(sp):
            for i, k in enumerate(("Wv", "Wq", "Wk")):
                sp.dma_start(Wvqk[:, i * D:(i + 1) * D], io[k]).then_inc(w_in, 16)
            for i, k in enumerate(("bv", "bq", "bk")):
                sp.dma_start(rows[:, i], io[k].partition_broadcast(P)).then_inc(w_in, 16)
            for r in range(3):
                sp.dma_start(bk3[r * C:(r + 1) * C], io["bk_c"]).then_inc(w_in, 16)
            sp.wait_ge(shift_copied, 2)
            sp.dma_start(io["shift"].rearrange("(a p) q -> p a q", a=2), shiftT[:]).then_inc(shift_out, 16)
            sp.wait_ge(shift_out, 16)

        @block.gpsimd
        def _(pool):
            chain = Chain(pool, pool_step)
            chain(pool.memset(Wk3[:, :, 3 * C:KROWS], 0.0))
            chain(pool.memset(bk3[3 * C:KROWS], 1.0))
            pool.sem_inc(w_made, 2)
            with pool.Fori(0, CHUNKS // 2) as cc:
                for b in range(2):
                    wait_apart(pool, xrow_made, 2 * cc + b + 1, pool_apart)
                    pool.tensor_copy(G["x1"][:, bass.ds((2 * cc + b) * TPC, TPC)], xrow[:, b]).then_inc(x1_stored, 1)
            pool.wait_ge(kpart, 1)
            pool.partition_all_reduce(kmax[:, 1], kmax[:, 0], P, bass.bass_isa.ReduceOp.max).then_inc(kall, 1)

        @block.tensor
        def _(pe):
            def turn(b):
                for s in range(TPC):
                    last = pe.transpose(xT_ps[:, b, s * P:(s + 1) * P], xrow[:, b, s], G["ident"][:])
                last.then_inc(xT_made, 1)

            pe.wait_ge(xrow_made, 1)
            turn(0)
            pe.wait_ge(w_made, 3)
            with pe.Fori(0, CHUNKS // 2) as cc:
                for b in range(2):
                    c = 2 * cc + b
                    pe.wait_ge(xT_copied, c + 1)
                    pe.wait_ge(xrow_made, c + 2)
                    turn(1 - b)
                    pe.wait_ge(v_taken, c + 1)
                    pe.wait_ge(kk_made, c + 1)
                    for s in range(TPC):
                        last = pe.matmul(nat_ps[:, s, 0:3 * D], xT[:, b, s * P:(s + 1) * P], Wvqk[:],
                                         start=True, stop=True)
                    last.then_inc(nat_made, 1)
                    for h in range(HEADS):
                        pe.wait_ge(k_low, c * HEADS + h + 1)
                        pe.matmul(k_ps[0:KROWS, h % 2], Wk3[:, h], xT[:, b],
                                  start=True, stop=True).then_inc(k_made, 1)
            pe.wait_ge(shift_made, 1)
            flat = shift[:].rearrange("p c h s -> p (c h s)")
            for a in range(2):
                pe.transpose(xT_ps[:, a, 0:P], flat[:, a * P:(a + 1) * P], G["ident"][:]).then_inc(shift_turned, 1)

        @block.scalar
        def _(act):
            def norm(n, b):
                for s in range(TPC):
                    t = (n % CHUNKS) * TPC + s
                    last = act.activation(xrow[:, b, s], G["x1"][:, bass.ds(t, 1)].rearrange("p a f -> p (a f)"),
                                          ACT.Identity, scale=G["rstd"][:, bass.ds(t, 1)],
                                          bias=G["nmr"][:, bass.ds(t, 1)])
                last.then_inc(xrow_made, 1)

            def copy_turned(n, b):
                act.wait_ge(xT_made, n + 1)
                act.activation(xT[:, b], xT_ps[:, b], ACT.Copy).then_inc(xT_copied, 1)

            act.wait_ge(w_in, 9 * 16)
            act.wait_ge(w_made, 3)
            act.sem_inc(kk_made, 1)
            for n in range(2):
                norm(n, n)
            copy_turned(0, 0)
            with act.Fori(0, CHUNKS // 2) as cc:
                for b in range(2):
                    c = 2 * cc + b
                    copy_turned(c + 1, 1 - b)
                    act.wait_ge(x1_stored, c + 1)
                    norm(c + 2, b)
                    for h in range(HEADS):
                        act.wait_ge(k_made, c * HEADS + h + 1)
                        act.activation(G["Kst"][:, h, bass.ds(c * CHUNK, CHUNK)], k_ps[0:KROWS, h % 2],
                                       ACT.Identity, bias=bk3[:, h:h + 1]).then_inc(k_high, 1)
                        if h == 0:
                            act.wait_ge(v_taken, c + 2)
                            act.wait_ge(dots_made, c + 1)
                            act.activation(prods[:, b, :, 2], nat_ps[:, :, 2 * D:3 * D], ACT.Square
                                           ).then_inc(kk_made, 1)
            for a in range(2):
                act.wait_ge(shift_turned, a + 1)
                act.activation(shiftT[:, a], xT_ps[:, a, 0:P], ACT.Copy).then_inc(shift_copied, 1)

        @block.vector
        def _(dve):
            chain = Chain(dve, step)
            dve.wait_ge(w_in, 9 * 16)
            for r in range(3):
                last = dve.tensor_copy(Wk3[:, :, r * C:(r + 1) * C], Wvqk[:, 2 * D:3 * D].rearrange("p (h c) -> p h c", h=HEADS))
            last.then_inc(w_made, 1)
            for start, n in ((v_taken, 1), (dots_made, 2), (k_low, 2)):
                dve.sem_inc(start, n)
            with dve.Fori(0, CHUNKS // 2) as cc:
                for b in range(2):
                    c = 2 * cc + b
                    row = lambda i: bcast(rows[:, i:i + 1], [P, TPC, D])
                    dve.wait_ge(nat_made, c + 1)
                    dve.wait_ge(dots_made, c + 1)
                    dve.tensor_tensor(qrow[:, b], nat_ps[:, :, D:2 * D], row(1), ALU.add).then_inc(q_made, 1)
                    dve.tensor_tensor(G["v"][:, bass.ds(c * TPC, TPC)], nat_ps[:, :, 0:D], row(0), ALU.add
                                      ).then_inc(v_taken, 1)
                    dve.wait_ge(q_made, c + 1)
                    for h in range(HEADS):
                        if h == 1:
                            dve.tensor_tensor(prods[:, b, :, 0], qrow[:, b], qrow[:, b], ALU.mult)
                        if h == 2:
                            dve.tensor_tensor(prods[:, b, :, 1], qrow[:, b], row(2), ALU.mult
                                              ).then_inc(prods_made, 1)
                        if h == 3:
                            dve.wait_ge(prods_made, c + 1)
                            dve.wait_ge(kk_made, c + 2)
                            dve.tensor_reduce(dots[:, bass.ds(c * TPC, TPC)].rearrange("p t a h -> p (t a h)"),
                                              prods[:, b].rearrange("p t a (h c) -> p (t a h) c", h=HEADS),
                                              AX.X, ALU.add).then_inc(dots_made, 1)
                        dve.wait_ge(k_high, c * HEADS + h + 1)
                        low = G["Kst"][C:2 * C, h, bass.ds(c * CHUNK, CHUNK)]
                        dve.scalar_tensor_tensor(out=low, in0=k_ps[C:2 * C, h % 2], scalar=bk3[C:2 * C, h:h + 1],
                                                 in1=low, op0=ALU.add, op1=ALU.subtract).then_inc(k_low, 1)
            dve.wait_ge(dots_made, CHUNKS + 2)
            dve.tensor_reduce(kmax[:, 0], dots[:, :, 2].rearrange("p t h -> p h t"), AX.X, ALU.max).then_inc(kpart, 1)
            dve.wait_ge(kall, 1)
            chain(dve.tensor_tensor(guard[:], dots[:, :, 0].rearrange("p t h -> p h t"),
                                    bcast(kmax[:, 1].unsqueeze(2), [P, HEADS, TILES]), ALU.mult))
            rsqrt_newton(chain, dve, root[:], guard[:], tmp[:])
            chain(dve.tensor_tensor(guard[:], guard[:], root[:], ALU.mult))
            chain(dve.tensor_tensor(guard[:], guard[:], dots[:, :, 1].rearrange("p t h -> p h t"), ALU.add))
            dve.tensor_scalar(shift[:].rearrange("p c h s -> p h c s"),
                              guard[:].rearrange("p h (c s) -> p h c s", s=TPC), -1.0, None, ALU.mult
                              ).then_inc(shift_made, 1)




def layer1(nc, io, G):
    NP = 4
    LAG = 3
    LOADS = 2
    HALF = 8
    TURNS = PAIRS // LOADS
    HS = TURNS * HALF
    EPI_STEPS = 15 + RSQRT_STEPS
    with ExitStack() as ctx:
        sb = lambda n, s, d=F32: ctx.enter_context(nc.sbuf_tensor(n, s, d))
        ps = lambda n, s, d=F32: ctx.enter_context(nc.psum_tensor(n, s, d))
        sem = lambda n: ctx.enter_context(nc.semaphore(n))
        adj = sb("adj1", [P, LOADS, 2, CHUNK])
        prob = sb("prob", [P, NP, 2, CHUNK])
        Qst = sb("Qst", [KROWS, 2, HEADS, CHUNK], FP16)
        xrow = sb("xrow1", [P, TPC, D])
        xT = sb("xT1", [P, CHUNK])
        skip = sb("skip", [P, 2, TPC, D])
        stage = sb("stage", [P, 2, HEADS, VW])
        Wq = sb("Wq_", [P, D])
        Wq3 = sb("Wq3", [P, HEADS, 3, C])
        Ws = sb("Ws_", [P, D])
        bq3 = sb("bq3", [3 * C, HEADS])
        bs = sb("bs_", [P, D])
        Wb = sb("Wb_", [P, 3, D])
        outT = sb("outT", [P, 2, CHUNK])
        att = sb("att", [P, TPC, D])
        diff = sb("diff", [P, TPC, D])
        gates = sb("gates", [P, TPC, 3, D])
        den = sb("den", [P, 2, TPC, HEADS])
        z = sb("z", [P, 2, TPC])
        stats = sb("stats1", [P, TPC, 6])
        mv = sb("mv1", [P, TPC, 2])
        rstd = sb("rstd", [P, 3, TPC])
        y = sb("y", [P, TPC, D])
        sc = ps("sc", [P, 2, 2, CHUNK])
        acc = ps("acc1", [P, 2, CHUNK])
        misc = ps("misc", [P, 2, CHUNK])
        adj_in = [sem(f"adj1_in{k}") for k in range(LOADS)]
        apart, pool_apart, y_free = sem("apart1"), sem("pool_apart"), sem("y_free")
        (w_in, w_made, scored, probed, masked, summed, staged, stage_init, acc_copied, turned,
         xrow_made, xT_made, xT_copied, q_made, q_high, q_low, skip_summed, skip_made, shift_in, step, att_made,
         z_made, ez_made, y_made, y_out, pool_step) = (sem(n) for n in (
             "w1_in", "w1_made", "scored", "probed", "masked", "summed", "staged", "stage_init", "acc_copied",
             "turned", "xrow1_made", "xT1_made", "xT1_copied", "q1_made", "q_high", "q_low",
             "skip_summed", "skip_made", "shift_in", "step1", "att_made", "z_made", "ez_made", "y_made", "y_out",
             "pool_step1"))
        out_rows = io["out"].rearrange("(p t) f -> p t f", p=P)
        shift_rows = io["shift"].rearrange("(c r) q -> c (r q)", c=CHUNKS)
        block = ctx.enter_context(nc.Block())

        RUNS = [(1, 3), (3, 4), (4, 6), (6, 8), (8, 9), (9, 10), (10, 11), (11, 12), (12, 13), (13, 14), (14, TURNS)]

        def runs(eng, turn_body, pieces):
            for (lo, hi), piece in zip(RUNS, pieces + [()] * (len(RUNS) - len(pieces))):
                with eng.Fori(lo, hi) as j:
                    turn_body(j)
                for part in piece:
                    part()
                if piece and eng is nc.vector:
                    eng.sem_inc(apart, 1)

        @block.sync
        def _(sp):
            for dst, src in ((Wq[:], io["Wq"]), (Ws[:], io["Ws"]), (bs[:], io["bs"].partition_broadcast(P)),
                             (Wb[:].rearrange("p a f -> p (a f)"),
                              io["Wb"].rearrange("a b -> (a b)").partition_broadcast(P))):
                sp.dma_start(dst, src).then_inc(w_in, 16)
            for r in range(3):
                sp.dma_start(bq3[r * C:(r + 1) * C], io["bq_c"]).then_inc(w_in, 16)
            with sp.Fori(0, CHUNKS * TURNS) as turn:
                for k in range(LOADS):
                    sp.wait_ge(masked, turn * HALF + 4 * k + 4)
                    sp.dma_start(adj[:, k].rearrange("p a w -> p (a w)"),
                                 io["adj"][bass.ds(turn * LOADS + k, 1)].rearrange("a p w -> (a p) w")
                                 ).then_inc(adj_in[k], 16)

        @block.gpsimd
        def _(pool):
            pool.memset(stage[:], 0.0).then_inc(pool_step, 1)
            pool.wait_ge(pool_step, 1)
            pool.memset(stage[:, :, :, C:C + 1], 1.0).then_inc(stage_init, 1)
            pool.dma_start(Qst[3 * C:KROWS, 0].rearrange("p h w -> p (h w)"), shift_rows[0:1]).then_inc(shift_in, 16)
            pool.wait_ge(stage_init, 1)
            pool.sem_inc(y_free, 1)

            def stage_values(c, lo, hi):
                with pool.Fori(lo, hi) as j:
                    for b in range(2):
                        wait_apart(pool, summed, (c * TILES + 2 * j + b) * 2 + 2, pool_apart)
                        pool.tensor_copy(stage[:, b, :, 0:C],
                                         G["v"][:, bass.ds(2 * j + b, 1)].rearrange("p a (h c) -> p (a h) c", h=HEADS)
                                         ).then_inc(staged, 1)

            def next_shift(c):
                pool.dma_start(Qst[3 * C:KROWS, bass.ds((c + 1) % 2, 1)].rearrange("p a h w -> p (a h w)"),
                               shift_rows[bass.ds((c + 1) % CHUNKS, 1)]).then_inc(shift_in, 16)

            def store(n):
                pool.wait_ge(y_made, n + 1)
                pool.dma_start(out_rows[:, bass.ds(n * TPC, TPC)], y[:]).then_inc(y_out, 16)

            stage_values(0, 0, 4)
            next_shift(0)
            stage_values(0, 4, TILES // 2)
            with pool.Fori(1, CHUNKS) as c:
                stage_values(c, 0, 4)
                next_shift(c)
                stage_values(c, 4, TILES // 2 - 1)
                store(c - 1)
                stage_values(c, TILES // 2 - 1, TILES // 2)
                pool.wait_ge(y_out, 16 * c)
                pool.sem_inc(y_free, 1)
            store(CHUNKS - 1)
            pool.wait_ge(shift_in, 16 * (CHUNKS + 1))
            pool.wait_ge(y_out, 16 * CHUNKS)

        @block.tensor
        def _(pe):
            def score(c, turn, k):
                pe.wait_ge(probed, c * HS + turn * HALF + k + 1)
                for hh in range(2):
                    h = 2 * (k % 2) + hh
                    last = pe.matmul(sc[:, k % 2, hh], G["Kst"][:, h, bass.ds((turn * (HALF // 2) + k // 2) * P, P)],
                                     Qst[:, bass.ds(c % 2, 1), h].rearrange("p a w -> p (a w)"),
                                     start=True, stop=True)
                last.then_inc(scored, 1)

            def weigh(c, turn, k, start=False, stop=False):
                pe.wait_ge(masked, c * HS + turn * HALF + k + HALF + 1)
                if k % 2 == 0:
                    pe.wait_ge(staged, c * TILES + turn * (HALF // 2) + k // 2 + 1)
                for hh in range(2):
                    last = pe.matmul(acc[hh * VW:(hh + 1) * VW, k % 2], stage[:, (k // 2) % 2, 2 * (k % 2) + hh],
                                     prob[:, k % NP, hh], start=start, stop=stop)
                last.then_inc(summed, 1)

            def step_of(c, turn, k):
                score(c, turn, k)
                weigh(c, turn if k >= LAG else turn - 1, (k - LAG) % HALF)

            def drain(c, k):
                weigh(c, TURNS - 1, HALF - LAG + k, stop=k >= LAG - 2)

            def turn_source(n):
                pe.wait_ge(xrow_made, n + 1)
                for s in range(TPC):
                    last = pe.transpose(misc[:, 0, s * P:(s + 1) * P], xrow[:, s], G["ident"][:])
                last.then_inc(xT_made, 1)

            def queries(n, heads):
                pe.wait_ge(xT_copied, n + 1)
                for h in heads:
                    if h >= 2:
                        pe.wait_ge(q_low, n * HEADS + h - 1)
                    pe.matmul(misc[0:3 * C, (h + 1) % 2], Wq3[:, h].rearrange("p a c -> p (a c)"), xT[:],
                              start=True, stop=True).then_inc(q_made, 1)

            def skips(n):
                pe.wait_ge(q_low, n * HEADS + HEADS)
                for s in range(TPC):
                    last = pe.matmul(misc[:, 1, s * P:(s + 1) * P], xT[:, s * P:(s + 1) * P], Ws[:],
                                     start=True, stop=True)
                last.then_inc(skip_summed, 1)

            def turn_out(n):
                pe.wait_ge(acc_copied, 2 * n + 4)
                for s in range(TPC):
                    for pair in range(2):
                        last = pe.transpose(misc[:, s // 2, (s % 2) * 2 * P + pair * P:(s % 2) * 2 * P + (pair + 1) * P],
                                            outT[:, pair, s * P:(s + 1) * P], G["ident"][:])
                last.then_inc(turned, 1)

            def chunk(c, first):
                pe.wait_ge(q_low, (c + 1) * HEADS)
                pe.wait_ge(shift_in, c * 16 + 16)
                for k in range(LAG):
                    score(c, 0, k)
                    if not first:
                        drain(c - 1, k)
                for k in range(LAG, HALF):
                    score(c, 0, k)
                    if k - LAG < 2:
                        if not first:
                            pe.wait_ge(acc_copied, 2 * c + k - LAG + 1)
                        weigh(c, 0, k - LAG, start=True)
                    else:
                        weigh(c, 0, k - LAG)

                def turn_body(j):
                    for k in range(HALF):
                        step_of(c, j, k)

                def after_epilogue():
                    if not first:
                        pe.wait_ge(att_made, c)
                runs(pe, turn_body, [
                    [] if first else [lambda: turn_out(c - 1)],
                    [after_epilogue, lambda: turn_source(c + 1)],
                    [lambda: queries(c + 1, (0, 1))],
                    [lambda: queries(c + 1, (2, 3))],
                    [lambda: skips(c + 1)],
                ])

            pe.sem_inc(summed, 4)
            pe.wait_ge(w_made, 1)
            turn_source(0)
            queries(0, range(HEADS))
            skips(0)
            chunk(0, True)
            with pe.Fori(1, CHUNKS) as c:
                chunk(c, False)
            for k in range(LAG):
                drain(CHUNKS - 1, k)
            turn_out(CHUNKS - 1)

        @block.scalar
        def _(act):
            def exps(c, j, k):
                act.wait_ge(scored, c * HS + j * HALF + k + 1)
                act.activation(prob[:, k % NP].rearrange("p a w -> p (a w)"),
                               sc[:, k % 2].rearrange("p a w -> p (a w)"), ACT.Exp, scale=SCALE
                               ).then_inc(probed, 1)

            def turn_body(c, j):
                for k in range(HALF):
                    exps(c, j, k)

            def copy_sums(n, pair):
                act.wait_ge(summed, (n + 1) * HS + 4 - 1 + pair)
                act.activation(outT[:, pair], acc[:, pair], ACT.Copy).then_inc(acc_copied, 1)

            def copy_source(n):
                act.wait_ge(skip_summed, n + 1)
                act.activation(xrow[:], G["x1"][:, bass.ds((n % CHUNKS) * TPC, TPC)], ACT.Copy).then_inc(xrow_made, 1)

            def copy_turned(n):
                act.wait_ge(xT_made, n + 1)
                act.activation(xT[:], misc[:, 0], ACT.Copy).then_inc(xT_copied, 1)

            def high(n, heads):
                for h in heads:
                    act.wait_ge(q_made, n * HEADS + h + 1)
                    act.activation(Qst[0:3 * C, bass.ds(n % 2, 1), h].rearrange("p a w -> p (a w)"),
                                   misc[0:3 * C, (h + 1) % 2], ACT.Identity, bias=bq3[:, h:h + 1]).then_inc(q_high, 1)

            def gate(n):
                act.wait_ge(z_made, n + 1)
                act.activation(z[:, 1], z[:, 0], ACT.Exp, scale=-1.0).then_inc(ez_made, 1)

            def chunk(c, first):
                for k in range(HALF):
                    exps(c, 0, k)
                    if not first and k in (LAG - 2, LAG - 1):
                        copy_sums(c - 1, k - (LAG - 2))
                runs(act, lambda j: turn_body(c, j), [
                    [lambda: copy_source(c + 1)],
                    [lambda: copy_turned(c + 1)],
                    [lambda: high(c + 1, (0, 1))],
                    [lambda: high(c + 1, (2, 3))],
                    [],
                    [] if first else [lambda: gate(c - 1)],
                ])

            act.sem_inc(probed, 2)
            act.sem_inc(acc_copied, 2)
            act.wait_ge(w_in, 7 * 16)
            copy_source(0)
            copy_turned(0)
            high(0, range(HEADS))
            chunk(0, True)
            with act.Fori(1, CHUNKS) as c:
                chunk(c, False)
            for pair in range(2):
                copy_sums(CHUNKS - 1, pair)
            gate(CHUNKS - 1)

        @block.vector
        def _(dve):
            def turn_body(c, j):
                for k in range(HALF):
                    dve.wait_ge(probed, c * HS + j * HALF + k + 3)
                    if k % 4 == 0:
                        dve.wait_ge(adj_in[k // 4], (c * TURNS + j) * 16 + 16)
                    m = (k // 2) % 2
                    dve.tensor_tensor(prob[:, k % NP], prob[:, k % NP],
                                      bcast(adj[:, k // 4, m:m + 1], [P, 2, CHUNK]), ALU.mult).then_inc(masked, 1)

            def low(n, heads):
                for h in heads:
                    dve.wait_ge(q_high, n * HEADS + h + 1)
                    rest = Qst[2 * C:3 * C, bass.ds(n % 2, 1), h].rearrange("p a w -> p (a w)")
                    dve.scalar_tensor_tensor(out=rest, in0=misc[2 * C:3 * C, (h + 1) % 2],
                                             scalar=bq3[2 * C:3 * C, h:h + 1], in1=rest, op0=ALU.add,
                                             op1=ALU.subtract).then_inc(q_low, 1)

            def skips(n):
                dve.wait_ge(skip_summed, n + 2)
                dve.tensor_tensor(skip[:, bass.ds(n % 2, 1)].rearrange("p a s f -> p (a s) f"),
                                  misc[:, 1].rearrange("p (s f) -> p s f", s=TPC),
                                  bcast(bs[:].unsqueeze(1), [P, TPC, D]), ALU.add).then_inc(skip_made, 1)

            def attention(chain, n):
                dve.wait_ge(turned, n + 1)
                sums = misc[:].rearrange("p b (s h w) -> p (b s h) w", h=HEADS, w=VW)
                chain(dve.tensor_copy(den[:, 0].rearrange("p s h -> p (s h)").unsqueeze(2), sums[:, :, C:C + 1]))
                chain(dve.tensor_scalar(den[:, 1], den[:, 0], 0.0, None, ALU.is_equal))
                chain(dve.tensor_tensor(den[:, 0], den[:, 0], den[:, 1], ALU.add))
                chain(dve.reciprocal(den[:, 1], den[:, 0]))
                dve.tensor_tensor(att[:].rearrange("p s (c h) -> p s h c", h=HEADS),
                                  misc[:].rearrange("p b (s h w) -> p (b s) h w", h=HEADS, w=VW)[:, :, :, 0:C],
                                  bcast(den[:, 1].unsqueeze(3), [P, TPC, HEADS, C]),
                                  ALU.mult).then_inc(att_made, 1)
                dve.wait_ge(att_made, n + 1)

            def gate_terms(chain, n, which):
                if which == 0:
                    dve.wait_ge(skip_made, n + 1)
                    chain(dve.tensor_tensor(diff[:], att[:], skip[:, bass.ds(n % 2, 1)].rearrange("p a s f -> p (a s) f"),
                                            ALU.subtract))
                part = (att[:], skip[:, bass.ds(n % 2, 1)].rearrange("p a s f -> p (a s) f"), diff[:])[which]
                chain(dve.tensor_tensor(gates[:, :, which], part, bcast(Wb[:, which:which + 1], [P, TPC, D]), ALU.mult))

            def gate_sum(chain, n):
                dve.tensor_reduce(z[:, 0], gates[:].rearrange("p s a f -> p s (a f)"), AX.X, ALU.add).then_inc(z_made, 1)

            def add_input(chain, n):
                chain(dve.tensor_tensor(att[:], att[:], G["x1"][:, bass.ds(n * TPC, TPC)], ALU.add))

            def mix(chain, n):
                dve.wait_ge(ez_made, n + 1)
                chain(dve.tensor_scalar(z[:, 1], z[:, 1], -1.0, -1.0, ALU.mult, ALU.add))
                chain(dve.reciprocal(z[:, 0], z[:, 1]))
                for s in range(TPC):
                    last = dve.scalar_tensor_tensor(out=att[:, s], in0=diff[:, s], scalar=z[:, 0, s:s + 1],
                                                    in1=att[:, s], op0=ALU.mult, op1=ALU.add)
                chain(last)

            def statistics(chain, n):
                for s in range(TPC):
                    last = dve.bn_stats(stats[:, s], att[:, s])
                chain(last)
                dve.sem_inc(apart, 1)
                for s in range(TPC):
                    last = dve.bn_aggr(mv[:, s], stats[:, s])
                chain(last)
                chain(dve.tensor_scalar(rstd[:, 0], mv[:, :, 1], EPS, None, ALU.add))

            def deviation(chain, n):
                rsqrt_newton(chain, dve, rstd[:, 1], rstd[:, 0], rstd[:, 2])

            def norm(chain, n):
                dve.wait_ge(y_free, n + 1)
                for s in range(TPC):
                    last = dve.tensor_scalar(y[:, s], att[:, s], mv[:, s, 0:1], rstd[:, 1, s:s + 1],
                                             ALU.subtract, ALU.mult)
                last.then_inc(y_made, 1)

            def chunk(c, first):
                turn_body(c, 0)
                n = c - 1
                chain = Chain(dve, step, None if first else n * EPI_STEPS)
                epi = lambda *parts: [] if first else [lambda p=p: p(chain, n) for p in parts]
                gates_of = lambda which: lambda ch, m: gate_terms(ch, m, which)
                runs(dve, lambda j: turn_body(c, j), [
                    epi(attention),
                    epi(gates_of(0)),
                    epi(gates_of(1)) + [lambda: low(c + 1, (0, 1))],
                    epi(gates_of(2)) + [lambda: low(c + 1, (2, 3))],
                    epi(gate_sum),
                    [lambda: skips(c + 1)] + epi(add_input),
                    epi(mix),
                    epi(statistics),
                    epi(deviation),
                    epi(norm),
                ])
                assert first or chain.steps == EPI_STEPS, chain.steps

            dve.sem_inc(masked, HALF)
            dve.wait_ge(w_in, 7 * 16)
            for r in range(3):
                last = dve.tensor_copy(Wq3[:, :, r], Wq[:].rearrange("p (h c) -> p h c", h=HEADS))
            last.then_inc(w_made, 1)
            dve.sem_inc(skip_summed, 1)
            low(0, range(HEADS))
            skips(0)
            chunk(0, True)
            with dve.Fori(1, CHUNKS) as c:
                chunk(c, False)
            n = CHUNKS - 1
            chain = Chain(dve, step, n * EPI_STEPS)
            attention(chain, n)
            for which in range(3):
                gate_terms(chain, n, which)
            gate_sum(chain, n)
            add_input(chain, n)
            mix(chain, n)
            statistics(chain, n)
            deviation(chain, n)
            norm(chain, n)


def program(nc, io):
    with ExitStack() as ctx:
        sb = lambda n, s, d=F32: ctx.enter_context(nc.sbuf_tensor(n, s, d))
        G = {"ident": sb("ident", [P, P]), "ones": sb("ones", [P, P]),
             "x1": sb("x1", [P, TILES, D]), "rstd": sb("rstd_", [P, TILES]), "nmr": sb("nmr", [P, TILES])}
        with ExitStack() as first:
            sb0 = lambda n, s, d=F32: first.enter_context(nc.sbuf_tensor(n, s, d))
            for n in ("f1", "neg_f2", "A", "Cf", "e1", "e2"):
                G[n] = sb0(n, [P, TILES])
            G["F1"] = sb0("F1", [P, N])
            G["XI"] = sb0("XI", [P, TILES, 3, ONE], BF16)
            G["XJ"] = sb0("XJ", [P, TILES, 2, ONE], FP16)
            G["SX"] = sb0("SX", [P, ONE])
            node_logits(nc, io, G)
            source_factors(nc, io, G)
            layer0(nc, io, G)
        G["Kst"] = sb("Kst", [KROWS, HEADS, N], FP16)
        G["v"] = sb("v", [P, TILES, D])
        projections(nc, io, G)
        layer1(nc, io, G)


_NAMES = {"x": "x", "inl": "L0_gnn_inlayer2", "W1": "L0_gnn_W1", "w2": "L0_gnn_w2", "w3": "L0_gnn_w3",
          "b2": "L0_gnn_b2", "b3": "L0_gnn_b3", "Wq": "L1_gnn_Wq", "bq": "L1_gnn_bq", "Wk": "L1_gnn_Wk",
          "bk": "L1_gnn_bk", "Wv": "L1_gnn_Wv", "bv": "L1_gnn_bv", "Ws": "L1_gnn_Ws", "bs": "L1_gnn_bs",
          "Wb": "L1_gnn_Wb"}


def kernel(**inputs):
    import numpy as np
    import concourse.bacc as bacc
    from concourse.bass_utils import run_bass_kernel_spmd

    arrays = {k: np.asarray(inputs[name]) for k, name in _NAMES.items()}
    for k in ("b2", "b3"):
        arrays[k] = arrays[k].reshape(1, 1)
    for k in ("bq", "bk"):
        arrays[k + "_c"] = arrays[k].reshape(HEADS, C).T
    adj = np.asarray(inputs["adj"]).reshape(P, CHUNKS, TPC, P, PAIRS, 2)
    arrays["adj"] = adj.transpose(1, 4, 3, 5, 2, 0).reshape(CHUNKS * PAIRS, P, PAIR_W)
    nc = bacc.Bacc("TRN2", target_bir_lowering=False, num_devices=1)
    io, sent = {}, {}
    for k, a in arrays.items():
        sent[f"in_{k}_dram"] = np.ascontiguousarray(a)
        io[k] = nc.dram_tensor(f"in_{k}_dram", a.shape, mybir.dt.from_np(a.dtype), kind="ExternalInput").ap()
    io["out"] = nc.dram_tensor("out_dram", (N, D), F32, kind="ExternalOutput").ap()
    io["shift"] = nc.dram_tensor("shift_dram", (CHUNKS * HEADS * TPC, P), FP16, kind="Internal").ap()
    program(nc, io)
    return run_bass_kernel_spmd(nc, [sent], core_ids=[0]).results[0]["out_dram"]
```
